# Optimizing a Trainium2 kernel written in Bass

```python
import numpy as np
import jax
import jax.numpy as jnp

def _softmax(x, axis=-1):
    return jax.nn.softmax(x, axis=axis)

def _gelu(x):
    return jax.nn.gelu(x, approximate=True)

def _silu(x):
    return jax.nn.silu(x)

def _sigmoid(x):
    return jax.nn.sigmoid(x)

def _layernorm(x, axis=-1, eps=1e-05):
    m = jnp.mean(x, axis=axis, keepdims=True)
    v = jnp.var(x, axis=axis, keepdims=True)
    return (x - m) / jnp.sqrt(v + eps)

def _scatter_add(tgt, idx, src, axis=0):
    return tgt.at[idx].add(src)

def _segment_sum(src, seg, n):
    return jax.ops.segment_sum(src, seg, n)
kernel_name = 'mk_recurrent_d1_jaxref_r4_833ebd'

def setup_inputs(seed: int=0):
    np.random.seed(seed)
    _w = jnp.asarray

    def _L0_attn_setup():
        import jax, jax.numpy as jnp
        import numpy as np
        B, S, HID = (2, 512, 512)
        H, HKV, D = (16, 4, 128)
        ROPE_BASE = 1000000.0
        EPS = 1e-05

        def _layernorm(x, g, b):
            mu = jnp.mean(x, axis=-1, keepdims=True)
            var = jnp.mean(jnp.square(x - mu), axis=-1, keepdims=True)
            return (x - mu) * jax.lax.rsqrt(var + EPS) * g + b

        def _rope_tables(seq_len, dim, base):
            inv_freq = 1.0 / base ** (jnp.arange(0, dim, 2, dtype=jnp.float32) / dim)
            t = jnp.arange(seq_len, dtype=jnp.float32)
            freqs = jnp.outer(t, inv_freq)
            cos = jnp.concatenate([jnp.cos(freqs), jnp.cos(freqs)], axis=-1)
            sin = jnp.concatenate([jnp.sin(freqs), jnp.sin(freqs)], axis=-1)
            return (cos, sin)

        def _rotate_half(x):
            x1, x2 = jnp.split(x, 2, axis=-1)
            return jnp.concatenate([-x2, x1], axis=-1)
        key = jax.random.key(seed)
        k1, k2, k3 = jax.random.split(key, 3)
        return {'x': jax.random.normal(k1, (B, S, HID), dtype=jnp.float32), 'w_qkv': jax.random.normal(k2, ((H + 2 * HKV) * D, HID), dtype=jnp.float32) * 0.02, 'w_o': jax.random.normal(k3, (HID, H * D), dtype=jnp.float32) * 0.02, 'qn_g': jnp.ones((D,), jnp.float32), 'qn_b': jnp.zeros((D,), jnp.float32), 'kn_g': jnp.ones((D,), jnp.float32), 'kn_b': jnp.zeros((D,), jnp.float32)}
    _L0_attn_in = _L0_attn_setup()

    def _L0_ffn_setup():
        import jax, jax.numpy as jnp
        import numpy as np
        DIM = 512
        HID = 1408
        ZERO_POINT = 128.0

        def _qlinear(x, wq, scale):
            W = (wq.astype(jnp.float32) - ZERO_POINT) * scale[:, None]
            return jnp.einsum('bsd,hd->bsh', x, W)
        key = jax.random.key(seed)
        ks = jax.random.split(key, 7)
        B, S = (4, 512)
        sg = jax.random.uniform(ks[1], (HID,)) * (0.02 / np.sqrt(DIM)) + 0.0001
        su = jax.random.uniform(ks[3], (HID,)) * (0.02 / np.sqrt(DIM)) + 0.0001
        sd = jax.random.uniform(ks[5], (DIM,)) * (0.02 / np.sqrt(HID)) + 0.0001
        return {'x': jax.random.normal(ks[0], (B, S, DIM), dtype=jnp.float32), 'wq_gate': jax.random.randint(ks[2], (HID, DIM), 0, 64, dtype=jnp.int32), 's_gate': sg, 'wq_up': jax.random.randint(ks[4], (HID, DIM), 0, 64, dtype=jnp.int32), 's_up': su, 'wq_down': jax.random.randint(ks[6], (DIM, HID), 0, 64, dtype=jnp.int32), 's_down': sd}
    _L0_ffn_in = _L0_ffn_setup()
    _d = {'L0_attn_x': _L0_attn_in['x'], 'L0_attn_w_qkv': _L0_attn_in['w_qkv'], 'L0_attn_w_o': _L0_attn_in['w_o'], 'L0_attn_qn_g': _L0_attn_in['qn_g'], 'L0_attn_qn_b': _L0_attn_in['qn_b'], 'L0_attn_kn_g': _L0_attn_in['kn_g'], 'L0_attn_kn_b': _L0_attn_in['kn_b'], 'L0_ffn_wq_gate': _L0_ffn_in['wq_gate'], 'L0_ffn_s_gate': _L0_ffn_in['s_gate'], 'L0_ffn_wq_up': _L0_ffn_in['wq_up'], 'L0_ffn_s_up': _L0_ffn_in['s_up'], 'L0_ffn_wq_down': _L0_ffn_in['wq_down'], 'L0_ffn_s_down': _L0_ffn_in['s_down']}
    _x0 = _d['L0_attn_x']
    _d['L0_attn_x'] = jax.random.normal(jax.random.fold_in(jax.random.key(seed), 1), (2, 1024, 512), dtype=_x0.dtype)
    del _x0
    return _d

def reference(L0_attn_x, L0_attn_w_qkv, L0_attn_w_o, L0_attn_qn_g, L0_attn_qn_b, L0_attn_kn_g, L0_attn_kn_b, L0_ffn_wq_gate, L0_ffn_s_gate, L0_ffn_wq_up, L0_ffn_s_up, L0_ffn_wq_down, L0_ffn_s_down):

    def _L0_attn_ref(x, w_qkv, w_o, qn_g, qn_b, kn_g, kn_b):
        import jax, jax.numpy as jnp
        import numpy as np
        B, S, HID = (2, 512, 512)
        H, HKV, D = (16, 4, 128)
        ROPE_BASE = 1000000.0
        EPS = 1e-05

        def _layernorm(x, g, b):
            mu = jnp.mean(x, axis=-1, keepdims=True)
            var = jnp.mean(jnp.square(x - mu), axis=-1, keepdims=True)
            return (x - mu) * jax.lax.rsqrt(var + EPS) * g + b

        def _rope_tables(seq_len, dim, base):
            inv_freq = 1.0 / base ** (jnp.arange(0, dim, 2, dtype=jnp.float32) / dim)
            t = jnp.arange(seq_len, dtype=jnp.float32)
            freqs = jnp.outer(t, inv_freq)
            cos = jnp.concatenate([jnp.cos(freqs), jnp.cos(freqs)], axis=-1)
            sin = jnp.concatenate([jnp.sin(freqs), jnp.sin(freqs)], axis=-1)
            return (cos, sin)

        def _rotate_half(x):
            x1, x2 = jnp.split(x, 2, axis=-1)
            return jnp.concatenate([-x2, x1], axis=-1)
        b, s, _ = x.shape
        qkv = jnp.einsum('bsh,oh->bso', x, w_qkv)
        q, k, v = jnp.split(qkv, [H * D, (H + HKV) * D], axis=-1)
        q = q.reshape(b, s, H, D).transpose(0, 2, 1, 3)
        k = k.reshape(b, s, HKV, D).transpose(0, 2, 1, 3)
        v = v.reshape(b, s, HKV, D).transpose(0, 2, 1, 3)
        q = _layernorm(q, qn_g, qn_b)
        k = _layernorm(k, kn_g, kn_b)
        cos, sin = _rope_tables(s, D, ROPE_BASE)
        q = q * cos + _rotate_half(q) * sin
        k = k * cos + _rotate_half(k) * sin
        rep = H // HKV
        k = jnp.repeat(k, rep, axis=1)
        v = jnp.repeat(v, rep, axis=1)
        scores = jnp.einsum('bhqd,bhkd->bhqk', q, k) / jnp.sqrt(jnp.float32(D))
        causal = jnp.triu(jnp.ones((s, s), dtype=bool), k=1)
        scores = jnp.where(causal, -jnp.inf, scores)
        weights = jax.nn.softmax(scores, axis=-1)
        attn = jnp.einsum('bhqk,bhkd->bhqd', weights, v)
        attn = attn.transpose(0, 2, 1, 3).reshape(b, s, H * D)
        return jnp.einsum('bsd,od->bso', attn, w_o)

    def _L0_ffn_ref(x, wq_gate, s_gate, wq_up, s_up, wq_down, s_down):
        import jax, jax.numpy as jnp
        import numpy as np
        DIM = 512
        HID = 1408
        ZERO_POINT = 128.0

        def _qlinear(x, wq, scale):
            W = (wq.astype(jnp.float32) - ZERO_POINT) * scale[:, None]
            return jnp.einsum('bsd,hd->bsh', x, W)
        gate = _qlinear(x, wq_gate, s_gate)
        gate = jax.nn.silu(gate)
        up = _qlinear(x, wq_up, s_up)
        return _qlinear(gate * up, wq_down, s_down)
    x = L0_attn_x
    xn = _layernorm(x, axis=-1)
    s = _L0_attn_ref(xn, L0_attn_w_qkv, L0_attn_w_o, L0_attn_qn_g, L0_attn_qn_b, L0_attn_kn_g, L0_attn_kn_b)
    g = _silu(_L0_ffn_ref(xn, L0_ffn_wq_gate, L0_ffn_s_gate, L0_ffn_wq_up, L0_ffn_s_up, L0_ffn_wq_down, L0_ffn_s_down))
    x = x + s * g
    return x

_drawn_inputs = setup_inputs


def setup_inputs(seed=0):
    import zlib

    import numpy as np

    out = dict(_drawn_inputs(seed))
    spreads = {'L0_attn_qn_g': (1.0, 0.6),
     'L0_attn_qn_b': (0.0, 0.8),
     'L0_attn_kn_g': (1.0, 0.6),
     'L0_attn_kn_b': (0.0, 0.8)}
    factors = {'L0_attn_w_qkv': 8.0,
     'L0_attn_w_o': 8.0,
     'L0_ffn_s_gate': 8.0,
     'L0_ffn_s_up': 8.0,
     'L0_ffn_s_down': 8.0}
    for name, (base, spread) in spreads.items():
        noise = np.random.default_rng([zlib.crc32(name.encode()), seed]).standard_normal(out[name].shape)
        drawn = base * np.exp(spread * noise) if base else spread * noise
        out[name] = jnp.asarray(drawn.astype(out[name].dtype))
    for name, factor in factors.items():
        out[name] = (out[name] * factor).astype(out[name].dtype)
    return out
```

```python
from contextlib import ExitStack

import concourse.bass as bass
from concourse import mybir

F32 = mybir.dt.float32
F32R = mybir.dt.float32r
BF16 = mybir.dt.bfloat16
I32 = mybir.dt.int32
ALU = mybir.AluOpType
ACT = mybir.ActivationFunctionType
AX_X = mybir.AxisListType.X

P = 128
B, S, DIM = 2, 1024, 512
H, HKV, D = 16, 4, 128
REP = H // HKV
HID = 1408
EPS = 1e-5
ZERO_POINT = 128.0
KC = DIM // P
NC = HID // P
TILES = B * S // P
TG = 4
TPG = TILES // TG
GTOK = TPG * P
QKV_TILES = (H + 2 * HKV)
NST = S // P
KV_COLS = (REP + 2) * D
QK_COLS = (REP + 1) * D


def ffn_events():
    first = [[] for _ in range(NC)]
    for c in range(NC - 1):
        first[c] = [("g", c + 1), ("u", c + 1), ("d", c + 1)]
    for t in range(TPG):
        first[2 + 2 * t].append(("x", t))
    for r in range(3):
        first[3 + 2 * r].append(("q", r))
    middle = [[] for _ in range(NC)]
    items = [("q", r) for r in range(7)] + [("o", h) for h in range(5)]
    for n, item in enumerate(items):
        middle[n * NC // len(items)].append(item)
    for t in range(TPG):
        middle[1 + 2 * t].append(("x", t))
    last = [[] for _ in range(NC)]
    items = [("q", r) for r in range(7)] + [("o", h) for h in range(6)]
    for n, item in enumerate(items):
        last[n * NC // len(items)].append(item)
    return first, middle, last


def ffn_block(nc, dram, scratch):
    x, wqkv, wo, wg, wu, wd, sg, su, sd = (
        dram[k] for k in ("x", "wqkv", "wo", "wg", "wu", "wd", "sg", "su", "sd"))
    xT_out, wqkvT_out, woT_out, gate_out = scratch
    FIRST, MIDDLE, LAST = ffn_events()
    prologue = [("x", t) for t in range(TPG)] + [("g", 0), ("u", 0), ("d", 0)]

    def slots(tg):
        return FIRST if isinstance(tg, int) and tg == 0 else LAST if isinstance(tg, int) and tg == TG - 1 else MIDDLE

    def flat(by_slot):
        return [e for slot in by_slot for e in slot]

    lists = {"pro": prologue, "first": flat(FIRST), "middle": flat(MIDDLE), "last": flat(LAST)}

    def count(events, kinds):
        return sum(e[0] in kinds for e in events)

    def before(tg, kinds):
        if isinstance(tg, int) and tg == 0:
            return count(prologue, kinds)
        return count(prologue, kinds) + count(lists["first"], kinds) + (tg - 1) * count(lists["middle"], kinds)

    RAW = "gudqo"
    STAGED = "qo"
    PRE = "gudx"
    RAW_RING, STAGE_RING, X_RING, H_RING, GU_RING = 2, 2, 2, 2, 3

    ctx = ExitStack()
    with ctx:
        def sb(name, shape, dt=F32):
            return ctx.enter_context(nc.sbuf_tensor(name, shape, dt))

        def sem(name):
            return ctx.enter_context(nc.semaphore(name))

        wgT = sb("wgT", [P, 2, KC, HID], F32R)
        wuT = sb("wuT", [P, 2, KC, HID], F32R)
        wdT = sb("wdT", [P, 2, NC, DIM], F32R)
        xT = sb("xT", [P, 2, TPG, 2, KC, P], F32R)
        hT = sb("hT", [P, H_RING, 2, GTOK], F32R)
        raw = sb("raw", [P, RAW_RING, DIM])
        stage = sb("stage", [P, STAGE_RING, 2, KC, P], F32R)
        xin = sb("xin", [P, X_RING, DIM])
        hf = sb("hf", [P, H_RING, GTOK])
        gbuf = sb("gbuf", [P, 2, DIM])
        sd_row = sb("sd_row", [P, DIM])
        s_col = sb("s_col", [P, 2, NC])
        ident = sb("ident", [P, P])
        stats = sb("stats", [P, X_RING, 6])
        moments = sb("moments", [P, X_RING, 2])
        veps = sb("veps", [P, X_RING, 1])
        rstd = sb("rstd", [P, X_RING, 1])
        minus_half = sb("minus_half", [P, 1])
        eps_col = sb("eps_col", [P, 1])
        touched = sb("touched", [P, 1])
        prep = ctx.enter_context(nc.psum_tensor("prep", [P, DIM], F32))
        gu = ctx.enter_context(nc.psum_tensor("gu", [P, GU_RING, GTOK], F32))
        y = ctx.enter_context(nc.psum_tensor("y", [P, TPG, DIM], F32))

        ident_zero = sem("ident_zero")
        ident_ready = sem("ident_ready")
        scales_in = sem("scales_in")
        raw_in = [sem(f"raw_in{i}") for i in range(RAW_RING)]
        x_in = [sem(f"x_in{i}") for i in range(X_RING)]
        stats_done = sem("stats_done")
        moments_done = sem("moments_done")
        veps_done = sem("veps_done")
        rstd_done = sem("rstd_done")
        pre_done = sem("pre_done")
        turned = sem("turned")
        hi_done = sem("hi_done")
        lo_done = sem("lo_done")
        stage_out = [sem(f"stage_out{i}") for i in range(STAGE_RING)]
        xT_stored = sem("xT_stored")
        gate_done = sem("gate_done")
        up_done = sem("up_done")
        silu_done = sem("silu_done")
        h_done = sem("h_done")
        hhi_done = sem("hhi_done")
        hlo_done = sem("hlo_done")
        down_done = sem("down_done")
        yscaled = sem("yscaled")
        g_done = sem("g_done")
        g_out = [sem(f"g_out{i}") for i in range(2)]

        def walk(tg):
            seen = []
            for c, events in enumerate(slots(tg)):
                for n, e in enumerate(events):
                    yield c, n, e, list(seen)
                    seen.append(e)

        def prologue_walk():
            for n, e in enumerate(prologue):
                yield 0, n, e, prologue[:n]

        def index(tg, seen, kinds="gudqox"):
            if tg is None:
                return count(seen, kinds)
            return before(tg, kinds) + count(seen, kinds)

        def ring(tg, seen, kinds, n):
            return count(seen, kinds) % n

        def uses(events, kinds, n, slot):
            return len(range(slot, count(events, kinds), n))

        def ring_uses(tg, seen, kinds, n, slot):
            within = uses(seen, kinds, n, slot)
            if tg is None:
                return within
            pro = uses(prologue, kinds, n, slot)
            if isinstance(tg, int) and tg == 0:
                return pro + within
            return (pro + uses(lists["first"], kinds, n, slot) + within
                    + (tg - 1) * uses(lists["middle"], kinds, n, slot))

        def previous(tg, seen, kinds, n):
            slot = ring(tg, seen, kinds, n)
            mine = [i for i, e in enumerate(seen) if e[0] in kinds]
            if len(mine) >= n:
                return (0 if tg is None else before(tg, "gudqox")) + mine[-n] + 1
            if tg is None:
                return None
            if isinstance(tg, int) and tg == 0:
                back, base = prologue, 0
            elif isinstance(tg, int) and tg == 1:
                back, base = lists["first"], before(0, "gudqox")
            else:
                return before(tg, "gudqox")
            mine = [i for i, e in enumerate(back) if e[0] in kinds]
            at = [i for k, i in enumerate(mine) if k % n == slot]
            return base + at[-1] + 1 if at else None

        def all_walks(engine, body):
            body(None)
            body(0)
            with engine.Fori(1, TG - 1) as tg:
                body(tg)
            body(TG - 1)

        block = ctx.enter_context(nc.Block())

        @block.gpsimd
        def _(pool):
            pool.memset(minus_half[:, :], -0.5).then_inc(ident_zero, 1)
            pool.memset(eps_col[:, :], EPS).then_inc(ident_zero, 1)
            pool.memset(ident[:, :], 0.0).then_inc(ident_zero, 1)
            pool.wait_ge(ident_zero, 3)
            pool.affine_select(out=ident[:, :], in_=ident[:, :], compare_op=ALU.not_equal, fill=1.0,
                               base=0, pattern=[[-1, P]], channel_multiplier=1).then_inc(ident_ready, 1)

            def rstd_of(n, slot):
                pool.wait_ge(moments_done, n + 1)
                pool.tensor_tensor(veps[:, slot, :], moments[:, slot, 1:2], eps_col[:, :], ALU.add).then_inc(veps_done, 1)
                pool.wait_ge(veps_done, n + 1)
                pool.tensor_tensor(rstd[:, slot, :], veps[:, slot, :], minus_half[:, :], ALU.pow).then_inc(rstd_done, 1)

            def low_of_h(n, s):
                pool.wait_ge(hhi_done, n + 1)
                pool.tensor_tensor(hT[:, s, 1, :], hf[:, s, :], hT[:, s, 0, :], ALU.subtract).then_inc(hlo_done, 1)

            def body(tg):
                events = prologue_walk() if tg is None else walk(tg)
                todo = {}
                for c, n, e, seen in events:
                    todo.setdefault(c, []).append((e, seen))
                for c in range(1 if tg is None else NC):
                    for e, seen in todo.get(c, []):
                        if e[0] == "x":
                            rstd_of(index(tg, seen, "x"), ring(tg, seen, "x", X_RING))
                    if tg is not None:
                        low_of_h(tg * NC + c, c % H_RING)

            all_walks(pool, body)

        @block.sync
        def _(sp):
            sp.dma_start(sd_row[:, :], sd.rearrange("(a n) -> a n", a=1).to_broadcast([P, DIM])).then_inc(scales_in, 16)
            with nc.allow_non_contiguous_dma(reason="two columns of scales, once"):
                sp.dma_start(s_col[:, 0, :], sg.rearrange("(c p) -> p c", p=P)).then_inc(scales_in, 16)
                sp.dma_start(s_col[:, 1, :], su.rearrange("(c p) -> p c", p=P)).then_inc(scales_in, 16)

            def load(tg, e, seen):
                kind, n = e
                prev = previous(tg, seen, "x" if kind == "x" else RAW, X_RING if kind == "x" else RAW_RING)
                if prev is not None:
                    sp.wait_ge(turned, prev)
                if kind == "x":
                    slot = ring(tg, seen, "x", X_RING)
                    tile = n if tg is None else (tg + 1) * TPG + n
                    sp.dma_start(xin[:, slot, :], x[tile]).then_inc(x_in[slot], 16)
                    return
                slot = ring(tg, seen, RAW, RAW_RING)
                done = 0 if tg is None or (isinstance(tg, int) and tg == 0) else before(tg, kind) if kind in "qo" else 0
                src = {"g": lambda: wg[n], "u": lambda: wu[n], "d": lambda: wd[n],
                       "q": lambda: wqkv[done + n], "o": lambda: wo[done + n]}[kind]()
                dst = raw[:, slot, :]
                if kind in "gud":
                    dst = dst.bitcast(I32)
                if kind in "do":
                    dst = dst.rearrange("p (r j) -> p r j", r=KC)
                sp.dma_start(dst, src).then_inc(raw_in[slot], 16)

            def store(tg, e, seen):
                kind, n = e
                if kind in STAGED:
                    slot = ring(tg, seen, STAGED, STAGE_RING)
                    done = 0 if isinstance(tg, int) and tg == 0 else before(tg, kind)
                    out = (wqkvT_out if kind == "q" else woT_out)[done + n]
                    sp.wait_ge(lo_done, index(tg, seen) + 1)
                    sp.dma_start(out, stage[:, slot].bitcast(F32)).then_inc(stage_out[slot], 16)
                if kind == "x" and n == TPG - 1:
                    group = 0 if tg is None else tg + 1
                    sp.wait_ge(lo_done, index(tg, seen) + 1)
                    sp.dma_start(xT_out[group], xT[:, group % 2].bitcast(F32)).then_inc(xT_stored, 16)

            def store_gate(tg, t):
                sp.wait_ge(g_done, tg * TPG + t + 1)
                sp.dma_start(gate_out[tg * TPG + t], gbuf[:, t % 2, :]).then_inc(g_out[t % 2], 16)

            def body(tg):
                events = [(c, e, seen) for c, _, e, seen in (prologue_walk() if tg is None else walk(tg))]
                for k in range(min(2, len(events))):
                    load(tg, *events[k][1:])
                at = 0
                for c in range(1 if tg is None else NC):
                    while at < len(events) and events[at][0] == c:
                        store(tg, *events[at][1:])
                        if at + 2 < len(events):
                            load(tg, *events[at + 2][1:])
                        at += 1
                    if c == 0 and tg is not None and not (isinstance(tg, int) and tg == 0):
                        for t in range(TPG):
                            store_gate(tg - 1, t)

            all_walks(sp, body)
            for t in range(TPG):
                store_gate(TG - 1, t)
            staged = lists["first"] + lists["middle"] * 2 + lists["last"]
            for slot in range(STAGE_RING):
                n = sum(uses(ev, STAGED, STAGE_RING, slot) * k
                        for ev, k in ((lists["first"], 1), (lists["middle"], TG - 2), (lists["last"], 1)))
                sp.wait_ge(stage_out[slot], 16 * n)
            sp.wait_ge(xT_stored, 16 * TG)
            for i in range(2):
                sp.wait_ge(g_out[i], 16 * TILES // 2)

        def destination(tg, e, seen, part):
            kind, n = e
            if kind == "x":
                parity = 0 if tg is None else (tg + 1) % 2
                return xT[:, parity, n, part]
            if kind in "gu":
                return (wgT if kind == "g" else wuT)[:, part, :, n * P:(n + 1) * P]
            if kind == "d":
                return wdT[:, part, n, :].rearrange("p (c n) -> p c n", c=KC)
            return stage[:, ring(tg, seen, STAGED, STAGE_RING), part]

        bank = prep[:, :].rearrange("p (c n) -> p c n", c=KC)

        @block.scalar
        def _(act):
            act.wait_ge(scales_in, 48)

            def high(tg, e, seen):
                i = index(tg, seen)
                kind, n = e
                if kind in STAGED:
                    slot = ring(tg, seen, STAGED, STAGE_RING)
                    used = ring_uses(tg, seen, STAGED, STAGE_RING, slot)
                    if not isinstance(used, int) or used > 0:
                        act.wait_ge(stage_out[slot], 16 * used)
                if kind == "x" and n == 0 and tg is not None:
                    if isinstance(tg, int) and tg == 0:
                        pass
                    else:
                        act.wait_ge(gate_done, tg * NC)
                        act.wait_ge(up_done, tg * NC)
                        act.wait_ge(xT_stored, 16 * tg)
                act.wait_ge(turned, i + 1)
                act.copy(destination(tg, e, seen, 0), bank).then_inc(hi_done, 1)

            def silu(tg, c):
                n = tg * NC + c
                act.wait_ge(gate_done, n + 1)
                if c >= H_RING:
                    act.wait_ge(hlo_done, n - H_RING + 1)
                elif not (isinstance(tg, int) and tg == 0):
                    act.wait_ge(hlo_done, tg * NC)
                act.activation(hf[:, c % H_RING, :], gu[:, (2 * c) % GU_RING, :], ACT.Silu,
                               scale=s_col[:, 0, c:c + 1]).then_inc(silu_done, 1)

            def high_of_h(tg, c):
                n = tg * NC + c
                act.wait_ge(h_done, n + 1)
                if c >= H_RING:
                    act.wait_ge(down_done, n - H_RING + 1)
                elif not (isinstance(tg, int) and tg == 0):
                    act.wait_ge(down_done, tg * NC - (1 - c) if c else tg * NC)
                act.copy(hT[:, c % H_RING, 0, :], hf[:, c % H_RING, :]).then_inc(hhi_done, 1)

            def gates(tg):
                for t in range(TPG):
                    act.wait_ge(yscaled, tg * TPG + t + 1)
                    act.activation(gbuf[:, t % 2, :], gbuf[:, t % 2, :], ACT.Silu).then_inc(g_done, 1)

            def body(tg):
                todo = {}
                for c, n, e, seen in (prologue_walk() if tg is None else walk(tg)):
                    todo.setdefault(c, []).append((e, seen))
                if tg is None:
                    for e, seen in todo[0]:
                        high(tg, e, seen)
                    return
                for c in range(NC):
                    events = todo.get(c, [])
                    for k, step in enumerate((lambda: silu(tg, c), lambda: high_of_h(tg, c), lambda: None, lambda: None)):
                        if k < len(events):
                            high(tg, *events[k])
                        step()
                    if c == 0 and not (isinstance(tg, int) and tg == 0):
                        gates(tg - 1)

            all_walks(act, body)
            gates(TG - 1)

        @block.vector
        def _(dve):
            def ready(tg, e, seen):
                kind, n = e
                if kind in "gud":
                    slot = ring(tg, seen, RAW, RAW_RING)
                    used = ring_uses(tg, seen, RAW, RAW_RING, slot)
                    dve.wait_ge(raw_in[slot], 16 * (used + 1))
                    dve.tensor_scalar(raw[:, slot, :], raw[:, slot, :].bitcast(I32), -ZERO_POINT, None,
                                      ALU.add).then_inc(pre_done, 1)
                if kind == "x":
                    slot = ring(tg, seen, "x", X_RING)
                    k = index(tg, seen, "x")
                    dve.wait_ge(x_in[slot], 16 * (ring_uses(tg, seen, "x", X_RING, slot) + 1))
                    dve.bn_stats(stats[:, slot, :], xin[:, slot, :]).then_inc(stats_done, 1)
                    dve.wait_ge(stats_done, k + 1)
                    dve.tensor_copy(touched[:, :], stats[:, slot, 0:1])
                    dve.bn_aggr(moments[:, slot, :], stats[:, slot, :]).then_inc(moments_done, 1)
                    dve.wait_ge(rstd_done, k + 1)
                    dve.tensor_scalar(xin[:, slot, :], xin[:, slot, :], moments[:, slot, 0:1], rstd[:, slot, :],
                                      ALU.subtract, ALU.mult).then_inc(pre_done, 1)

            def low(tg, e, seen):
                dve.wait_ge(hi_done, index(tg, seen) + 1)
                dve.tensor_tensor(destination(tg, e, seen, 1), bank, destination(tg, e, seen, 0),
                                  ALU.subtract).then_inc(lo_done, 1)

            def gated(tg, c):
                n = tg * NC + c
                dve.wait_ge(up_done, n + 1)
                dve.wait_ge(silu_done, n + 1)
                dve.scalar_tensor_tensor(hf[:, c % H_RING, :], gu[:, (2 * c + 1) % GU_RING, :], s_col[:, 1, c:c + 1],
                                         hf[:, c % H_RING, :], ALU.mult, ALU.mult).then_inc(h_done, 1)

            def scale_y(tg):
                dve.wait_ge(down_done, (tg + 1) * NC)
                for t in range(TPG):
                    if t >= 2 or not (isinstance(tg, int) and tg == 0):
                        dve.wait_ge(g_out[t % 2], 16 * (tg * (TPG // 2) + t // 2))
                    dve.tensor_tensor(gbuf[:, t % 2, :], y[:, t, :], sd_row[:, :], ALU.mult).then_inc(yscaled, 1)

            def body(tg):
                todo = {}
                events = [(c, e, seen) for c, _, e, seen in (prologue_walk() if tg is None else walk(tg))]
                for c, e, seen in events:
                    todo.setdefault(c, []).append((e, seen))
                following = [(e, seen) for _, e, seen in events][1:]
                if tg is None:
                    ready(tg, *todo[0][0])
                    for e, seen in todo[0]:
                        if following:
                            ready(tg, *following.pop(0))
                        low(tg, e, seen)
                    return
                ready(tg, *events[0][1:])
                for c in range(NC):
                    slot_events = todo.get(c, [])
                    for k in range(4):
                        if k < len(slot_events):
                            if following:
                                ready(tg, *following.pop(0))
                            low(tg, *slot_events[k])
                        if k == 1:
                            gated(tg, c)
                    if c == 0 and not (isinstance(tg, int) and tg == 0):
                        scale_y(tg - 1)

            dve.wait_ge(scales_in, 48)
            all_walks(dve, body)
            scale_y(TG - 1)

        @block.tensor
        def _(pe):
            pe.wait_ge(ident_ready, 1)

            def turn(tg, e, seen):
                kind, n = e
                if kind in PRE:
                    pe.wait_ge(pre_done, index(tg, seen, PRE) + 1)
                else:
                    slot = ring(tg, seen, RAW, RAW_RING)
                    pe.wait_ge(raw_in[slot], 16 * (ring_uses(tg, seen, RAW, RAW_RING, slot) + 1))
                i = index(tg, seen)
                if not (isinstance(i, int) and i == 0):
                    pe.wait_ge(lo_done, i)
                src = xin[:, ring(tg, seen, "x", X_RING), :] if kind == "x" else raw[:, ring(tg, seen, RAW, RAW_RING), :]
                for k in range(KC):
                    last = pe.transpose(prep[:, k * P:(k + 1) * P], src[:, k * P:(k + 1) * P], ident[:, :])
                last.then_inc(turned, 1)

            def hidden(tg, c, side):
                w = (wgT, wuT)[side]
                use = 2 * c + side
                if use >= GU_RING:
                    n = tg * NC + (use - GU_RING) // 2
                    pe.wait_ge(silu_done if (use - GU_RING) % 2 == 0 else h_done, n + 1)
                elif not (isinstance(tg, int) and tg == 0):
                    pe.wait_ge(silu_done, tg * NC)
                    pe.wait_ge(h_done, tg * NC)
                out = gu[:, use % GU_RING, :].rearrange("p (t n) -> p t n", t=TPG)
                parity = tg % 2
                for k in range(KC):
                    for wp, xp in ((0, 0), (0, 1), (1, 0)):
                        last = pe.matmul(out, w[:, wp, k, c * P:(c + 1) * P], xT[:, parity, :, xp, k, :],
                                         start=(k == 0 and wp == xp == 0), stop=(k == KC - 1 and wp == 1))
                last.then_inc(up_done if side else gate_done, 1)

            def down(tg, c):
                pe.wait_ge(hlo_done, tg * NC + c + 1)
                if c == 0 and not (isinstance(tg, int) and tg == 0):
                    pe.wait_ge(yscaled, tg * TPG)
                for t in range(TPG):
                    for hp, wp in ((0, 0), (0, 1), (1, 0)):
                        last = pe.matmul(y[:, t, :], hT[:, c % H_RING, hp, t * P:(t + 1) * P], wdT[:, wp, c, :],
                                         start=(c == 0 and hp == wp == 0), stop=(c == NC - 1 and hp == 1))
                last.then_inc(down_done, 1)

            def body(tg):
                todo = {}
                for c, n, e, seen in (prologue_walk() if tg is None else walk(tg)):
                    todo.setdefault(c, []).append((e, seen))
                if tg is None:
                    for e, seen in todo[0]:
                        turn(tg, e, seen)
                    pe.wait_ge(lo_done, len(prologue))
                    return
                for c in range(NC):
                    events = todo.get(c, [])
                    if c == 0:
                        pe.wait_ge(lo_done, before(tg, "gudqox"))
                    elif isinstance(tg, int) and tg == 0:
                        pe.wait_ge(lo_done, before(0, "gudqox") + sum(len(s) for s in FIRST[:c]))
                    steps = [lambda: hidden(tg, c, 0), lambda: hidden(tg, c, 1)]
                    if c > 0:
                        steps.append(lambda: down(tg, c - 1))
                    elif not (isinstance(tg, int) and tg == 0):
                        steps.append(lambda: down(tg - 1, NC - 1))
                    else:
                        steps.append(lambda: None)
                    for k, step in enumerate(steps):
                        if k < len(events):
                            turn(tg, *events[k])
                        step()
                    if len(events) > 3:
                        turn(tg, *events[3])

            all_walks(pe, body)
            down(TG - 1, NC - 1)


def schedule():
    steps = []
    for n in range(NST):
        steps += [("qkv", n), ("norm", n)]
        if n >= 1:
            steps.append(("rope", n - 1))
        if n >= 2:
            steps.append(("turn", n - 2))
    steps += [("rope", NST - 1), ("S", 0, 0), ("turn", NST - 2), ("S", 0, 1), ("turn", NST - 1), ("S", 0, 2), ("S", 0, 3)]
    blocks = [(u, j) for u in range(2 * REP) for j in range(blocks_of(u))]
    for k, (u, j) in enumerate(blocks):
        steps.append(("T", u, j))
        if u + 1 < 2 * REP:
            where = (0, 0, 1, 1) if blocks_of(u) == 4 else (0, 1, 2, 4)
            steps += [("S", u + 1, t) for t in range(4) if where[t] == j]
        if u == REP and j in (2, 3, 4, 5):
            steps.append(("out", j - 2))
        if k >= LAG:
            steps.append(("PV", *blocks[k - LAG]))
    steps += [("PV", *b) for b in blocks[-LAG:]]
    steps += [("out", 4 + t) for t in range(4)]
    return steps


LAG = 2
QT = 4
UNITS = 2 * REP


def blocks_of(u):
    return QT * (u // REP + 1)


def blocks_before(u):
    return sum(blocks_of(v) for v in range(u))


BLOCKS = blocks_before(UNITS)
PT_RING = 3
MASKED = -3.0e38


def attention_block(nc, dram, scratch, out):
    x, cos, ssin, norms, swapped = (dram[k] for k in ("x", "cos", "ssin", "norms", "norms_swapped"))
    xT_in, wqkvT_in, woT_in, gate_in = scratch
    STEPS = schedule()
    ctx = ExitStack()
    with ctx:
        def sb(name, shape, dt=F32):
            return ctx.enter_context(nc.sbuf_tensor(name, shape, dt))

        def sem(name):
            return ctx.enter_context(nc.semaphore(name))

        wT = sb("wT", [P, 2, KC, KV_COLS], F32R)
        woT = sb("woT", [P, 2, REP, DIM], F32R)
        xt = sb("xt", [P, 2, 2, KC, P], F32R)
        qk = sb("qk", [P, 2, REP + 1, S], F32R)
        v = sb("v", [P, 2, NST, D], F32R)
        pbuf = sb("pbuf", [P, 2, QT, S])
        pT = sb("pT", [P, PT_RING, 2, QT * P], F32R)
        aT = sb("aT", [P, 2, REP, QT * P], F32R)
        yacc = sb("yacc", [P, NST, DIM])
        tabs = sb("tabs", [P, 2, 3, NST, D])
        xg = sb("xg", [P, 2, 2, DIM])
        ident = sb("ident2", [P, P])
        identb = sb("identb", [P, P], BF16)
        mask = sb("mask", [P, P])
        maskb = sb("maskb", [P, P], BF16)
        zeros = sb("zeros", [P, P])
        stats = sb("stats2", [P, 2, REP + 1, 6])
        moments = sb("moments2", [P, 2, REP + 1, 2])
        veps = sb("veps2", [P, 2, REP + 1])
        rstd = sb("rstd2", [P, 2, REP + 1])
        nbias = sb("nbias", [P, 2, REP + 1])
        minus_half = sb("minus_half2", [P, 1])
        minus_one = sb("minus_one", [P, 1])
        eps_col = sb("eps_col2", [P, 1])
        touched = sb("touched2", [P, 2])
        nmax = sb("nmax", [P, 2, QT])
        lsum = sb("lsum", [P, 2, QT])
        linv = sb("linv", [P, 2, QT])

        work = pbuf[:, 1].rearrange("p a b -> p (a b)")

        def normed(n):
            return work[:, (n % 2) * 2048:(n % 2) * 2048 + QK_COLS]

        def rotated(n):
            return work[:, (n % 2) * 2048 + QK_COLS:(n % 2) * 2048 + 2 * QK_COLS]

        def roped(n):
            return work[:, (n % 2) * 2048 + 2 * QK_COLS:(n % 2) * 2048 + 3 * QK_COLS]

        made = pbuf[:, 0].rearrange("p a b -> p (a b)")
        cos_sb = made[:, 0:NST * D].rearrange("p (t d) -> p t d", d=D)
        sin_sb = made[:, NST * D:2 * NST * D].rearrange("p (t d) -> p t d", d=D)
        rows = made[:, 2 * NST * D:2 * NST * D + 8 * D].rearrange("p (a d) -> p a d", d=D)
        temp = made[:, 3 * NST * D:4 * NST * D].rearrange("p (t d) -> p t d", d=D)

        s_ps = ctx.enter_context(nc.psum_tensor("s_ps", [P, 2, S], F32))
        t_ps = ctx.enter_context(nc.psum_tensor("t_ps", [P, 2, QT * P], F32))
        o_ps = ctx.enter_context(nc.psum_tensor("o_ps", [P, 2, QT * P], F32))

        consts_made = sem("consts_made")
        consts_ready = sem("consts_ready")
        tables_in = sem("tables_in")
        tables_step = sem("tables_step")
        w_in = sem("w_in")
        wo_in = sem("wo_in")
        xt_in = [sem(f"xt_in{i}") for i in range(2)]
        qkv_done = sem("qkv_done")
        stats_done = sem("stats_done2")
        moments_done = sem("moments_done2")
        veps_done = sem("veps_done2")
        rstd_done = sem("rstd_done2")
        nbias_done = sem("nbias_done")
        norm_done = sem("norm_done")
        vhi_done = sem("vhi_done")
        vlo_done = sem("vlo_done")
        rot_made = sem("rot_made")
        rot_done = sem("rot_done")
        cosed = sem("cosed")
        rope_done = sem("rope_done")
        turned = sem("turned2")
        qkhi_done = sem("qkhi_done")
        qklo_done = sem("qklo_done")
        s_done = sem("s_done")
        max_done = sem("max_done")
        exp_done = sem("exp_done")
        linv_done = sem("linv_done")
        p_done = sem("p_done")
        pt_turned = sem("pt_turned")
        pthi_done = sem("pthi_done")
        ptlo_done = sem("ptlo_done")
        pv_done = sem("pv_done")
        ahi_done = sem("ahi_done")
        alo_done = sem("alo_done")
        out_done = sem("out_done")
        added = sem("added")
        yzero = sem("yzero")
        xg_in = [sem(f"xg_in{i}") for i in range(2)]
        mixed = sem("mixed")
        fin_done = sem("fin_done")
        stored = sem("stored")

        def head_steps(engine, body, after=None):
            with engine.Fori(0, B) as b:
                with engine.Fori(0, HKV) as kv:
                    body(b * HKV + kv)
                if after:
                    after(b)

        def cols(t, u):
            return (QT * (u // REP) + t + 1) * P

        def first_col(u, j):
            r = j - QT * (u // REP)
            return min(max(r, 0), 2) * P

        def pair(n):
            both = (t_ps, o_ps)[n % 2][:, :, :].rearrange("p a b -> p (a b)")
            return both[:, 0:QK_COLS].rearrange("p (h t) -> p h t", t=P)

        def out_bank(i):
            return 1 if i < QT else i % 2

        block = ctx.enter_context(nc.Block())

        @block.sync
        def _(sp):
            sp.sem_inc(stored, 1)
            sp.dma_start(cos_sb, cos).then_inc(tables_in, 16)
            sp.dma_start(sin_sb, ssin).then_inc(tables_in, 16)
            sp.dma_start(rows[:, 0:4, :], norms.rearrange("(o a) d -> o a d", o=1).to_broadcast([P, 4, D])).then_inc(tables_in, 16)
            sp.dma_start(rows[:, 4:8, :], swapped.rearrange("(o a) d -> o a d", o=1).to_broadcast([P, 4, D])).then_inc(tables_in, 16)

            def load_w(b, kv):
                it = b * HKV + kv
                sp.wait_ge(qkv_done, 2 + it * NST)
                for s, tile in enumerate([kv * REP + h for h in range(REP)] + [H + kv, H + HKV + kv]):
                    sp.dma_start(wT[:, :, :, s * D:(s + 1) * D].bitcast(F32), wqkvT_in[tile]).then_inc(w_in, 16)

            def load_x(b, kv, n):
                it = b * HKV + kv
                sp.wait_ge(qkv_done, 2 + it * NST + n - 1)
                sp.dma_start(xt[:, n % 2].bitcast(F32), xT_in[b * (TG // B) + n // TPG, :, n % TPG]).then_inc(xt_in[n % 2], 16)

            def load_wo(b, kv):
                sp.wait_ge(out_done, 1 + (b * HKV + kv) * NST)
                for h in range(REP):
                    sp.dma_start(woT[:, :, h, :].bitcast(F32), woT_in[kv * REP + h]).then_inc(wo_in, 16)

            def rest(b, kv):
                load_wo(b, kv)
                for n in range(2, NST):
                    load_x(b, kv, n)

            def begin(b, kv):
                load_w(b, kv)
                load_x(b, kv, 0)
                load_x(b, kv, 1)

            def results(b):
                def load(t):
                    if b or t >= 2:
                        sp.wait_ge(fin_done, b * NST + t - 1 if t >= 2 else b * NST)
                    sp.dma_start(xg[:, t % 2, 0, :], x[b * NST + t]).then_inc(xg_in[t % 2], 16)
                    sp.dma_start(xg[:, t % 2, 1, :], gate_in[b * NST + t]).then_inc(xg_in[t % 2], 16)

                load(0)
                load(1)
                for t in range(NST):
                    sp.wait_ge(fin_done, b * NST + t + 1)
                    sp.dma_start(out[b * NST + t], yacc[:, t, :]).then_inc(stored, 16)
                    if t + 2 < NST:
                        load(t + 2)

            begin(0, 0)
            for b in range(B):
                with sp.Fori(0, HKV - 1) as kv:
                    rest(b, kv)
                    begin(b, kv + 1)
                rest(b, HKV - 1)
                if b + 1 < B:
                    begin(b + 1, 0)
                results(b)
            sp.wait_ge(stored, 1 + 16 * B * NST)

        @block.gpsimd
        def _(pool):
            pool.memset(ident[:, :], 0.0).then_inc(consts_made, 1)
            pool.memset(mask[:, :], 0.0).then_inc(consts_made, 1)
            pool.memset(zeros[:, :], 0.0).then_inc(consts_made, 1)
            pool.memset(minus_half[:, :], -0.5).then_inc(consts_made, 1)
            pool.memset(minus_one[:, :], -1.0).then_inc(consts_made, 1)
            pool.memset(eps_col[:, :], EPS).then_inc(consts_made, 1)
            pool.wait_ge(consts_made, 6)
            pool.affine_select(out=ident[:, :], in_=ident[:, :], compare_op=ALU.not_equal, fill=1.0,
                               base=0, pattern=[[-1, P]], channel_multiplier=1).then_inc(consts_made, 1)
            pool.affine_select(out=mask[:, :], in_=mask[:, :], compare_op=ALU.is_ge, fill=MASKED,
                               base=0, pattern=[[-1, P]], channel_multiplier=1).then_inc(consts_made, 1)
            pool.wait_ge(consts_made, 8)
            pool.tensor_copy(identb[:, :], ident[:, :]).then_inc(consts_ready, 1)
            pool.tensor_copy(maskb[:, :], mask[:, :]).then_inc(consts_ready, 1)

            def halves(view):
                return view.rearrange("p (h s d) -> p h s d", s=2, d=D // 2)

            def body(it):
                for kind, *a in STEPS:
                    if kind == "norm":
                        n, = a
                        pool.wait_ge(moments_done, it * NST + n + 1)
                        pool.tensor_tensor(veps[:, n % 2, :], moments[:, n % 2, :, 1],
                                           eps_col[:, :].to_broadcast([P, REP + 1]), ALU.add).then_inc(veps_done, 1)
                        pool.wait_ge(veps_done, it * NST + n + 1)
                        pool.tensor_tensor(rstd[:, n % 2, :], veps[:, n % 2, :],
                                           minus_half[:, :].to_broadcast([P, REP + 1]), ALU.pow).then_inc(rstd_done, 1)
                    if kind == "rope":
                        n, = a
                        pool.wait_ge(norm_done, it * NST + n + 1)
                        src, dst = halves(normed(n)), halves(rotated(n))
                        for side, h0, h1 in ((0, 0, REP), (1, REP, REP + 1)):
                            for s in range(2):
                                t = tabs[:, side, 1, n:n + 1, s * (D // 2):(s + 1) * (D // 2)]
                                last = pool.tensor_tensor(dst[:, h0:h1, s, :], src[:, h0:h1, 1 - s, :],
                                                          t.to_broadcast([P, h1 - h0, D // 2]), ALU.mult)
                        last.then_inc(rot_made, 1)
                        pool.wait_ge(rot_made, it * NST + n + 1)
                        whole = rotated(n).rearrange("p (h d) -> p h d", d=D)
                        for side, h0, h1 in ((0, 0, REP), (1, REP, REP + 1)):
                            last = pool.tensor_tensor(whole[:, h0:h1, :], whole[:, h0:h1, :],
                                                      tabs[:, side, 2, n:n + 1, :].to_broadcast([P, h1 - h0, D]), ALU.add)
                        last.then_inc(rot_done, 1)
                    if kind == "S":
                        u, t = a
                        k = it * UNITS * QT + u * QT + t
                        pool.wait_ge(exp_done, k + 1)
                        pool.tensor_tensor(linv[:, u % 2, t:t + 1], lsum[:, u % 2, t:t + 1], minus_one[:, :],
                                           ALU.pow).then_inc(linv_done, 1)
                        pool.wait_ge(linv_done, k + 1)
                        w = pbuf[:, u % 2, t, 0:cols(t, u)]
                        pool.tensor_tensor(w, w, linv[:, u % 2, t:t + 1].to_broadcast([P, cols(t, u)]),
                                           ALU.mult).then_inc(p_done, 1)

            with pool.Fori(0, B) as b:
                pool.wait_ge(stored, 1 + b * (16 * NST))
                pool.tensor_tensor(touched[:, 1:2], minus_one[:, :], minus_one[:, :], ALU.add)
                pool.memset(yacc[:, :, :], 0.0).then_inc(yzero, 1)
                with pool.Fori(0, HKV) as kv:
                    body(b * HKV + kv)

        @block.scalar
        def _(act):
            def body(it):
                for kind, *a in STEPS:
                    if kind == "qkv":
                        n, = a
                        act.wait_ge(qkv_done, 2 + it * NST + n + 1)
                        act.copy(v[:, 0, n, :], s_ps[:, n % 2, QK_COLS:KV_COLS]).then_inc(vhi_done, 1)
                    if kind == "norm":
                        n, = a
                        act.wait_ge(nbias_done, it * NST + n + 1)
                        for h in range(REP + 1):
                            last = act.activation(normed(n)[:, h * D:(h + 1) * D], s_ps[:, n % 2, h * D:(h + 1) * D],
                                                  ACT.Identity, bias=nbias[:, n % 2, h:h + 1], scale=rstd[:, n % 2, h:h + 1])
                        last.then_inc(norm_done, 1)
                    if kind == "turn":
                        n, = a
                        act.wait_ge(turned, it * NST + n + 1)
                        act.copy(qk[:, 0, :, n * P:(n + 1) * P], pair(n)).then_inc(qkhi_done, 1)
                    if kind == "S":
                        u, t = a
                        act.wait_ge(max_done, it * UNITS * QT + u * QT + t + 1)
                        act.activation(pbuf[:, u % 2, t, 0:cols(t, u)], s_ps[:, t % 2, 0:cols(t, u)], ACT.Exp,
                                       bias=nmax[:, u % 2, t:t + 1], scale=1.0,
                                       accum_out=lsum[:, u % 2, t:t + 1]).then_inc(exp_done, 1)
                    if kind == "T":
                        u, j = a
                        k, c = blocks_before(u) + j, first_col(u, j)
                        act.wait_ge(pt_turned, it * BLOCKS + k + 1)
                        act.copy(pT[:, k % PT_RING, 0, c:], t_ps[:, k % 2, c:]).then_inc(pthi_done, 1)
                    if kind == "PV" and a[1] == blocks_of(a[0]) - 1:
                        u = a[0]
                        act.wait_ge(pv_done, it * UNITS + u + 1)
                        act.copy(aT[:, 0, u % REP, :], o_ps[:, u % 2, :]).then_inc(ahi_done, 1)

            head_steps(act, body)

        @block.vector
        def _(dve):
            dve.sem_inc(added, 1)
            dve.wait_ge(tables_in, 64)
            steps = [0]

            def link(made_by):
                steps[0] += 1
                made_by.then_inc(tables_step, 1)
                dve.wait_ge(tables_step, steps[0])

            def row(i):
                return rows[:, i:i + 1, :].to_broadcast([P, NST, D])

            link(dve.tensor_scalar(rows[:, 0:2, :], rows[:, 0:2, :], D ** -0.5, None, ALU.mult))
            link(dve.tensor_scalar(rows[:, 4:6, :], rows[:, 4:6, :], D ** -0.5, None, ALU.mult))
            for side in range(2):
                dve.tensor_tensor(tabs[:, side, 0], cos_sb, row(2 * side), ALU.mult)
                dve.tensor_tensor(tabs[:, side, 1], sin_sb, row(4 + 2 * side), ALU.mult)
                dve.tensor_tensor(tabs[:, side, 2], cos_sb, row(1 + 2 * side), ALU.mult)
                link(dve.tensor_tensor(temp, sin_sb, row(5 + 2 * side), ALU.mult))
                link(dve.tensor_tensor(tabs[:, side, 2], tabs[:, side, 2], temp, ALU.add))

            def body(it):
                for kind, *a in STEPS:
                    if kind == "norm":
                        n, = a
                        dve.wait_ge(qkv_done, 2 + it * NST + n + 1)
                        for h in range(REP + 1):
                            if h == REP:
                                dve.wait_ge(vhi_done, it * NST + n + 1)
                            last = dve.bn_stats(stats[:, n % 2, h, :], s_ps[:, n % 2, h * D:(h + 1) * D])
                        last.then_inc(stats_done, 1)
                        dve.wait_ge(stats_done, it * NST + n + 1)
                        dve.tensor_tensor(v[:, 1, n, :], s_ps[:, n % 2, QK_COLS:KV_COLS], v[:, 0, n, :],
                                          ALU.subtract).then_inc(vlo_done, 1)
                        for h in range(REP + 1):
                            last = dve.bn_aggr(moments[:, n % 2, h, :], stats[:, n % 2, h, :])
                        last.then_inc(moments_done, 1)
                        dve.wait_ge(rstd_done, it * NST + n + 1)
                        dve.scalar_tensor_tensor(nbias[:, n % 2, :], moments[:, n % 2, :, 0], -1.0, rstd[:, n % 2, :],
                                                 ALU.mult, ALU.mult).then_inc(nbias_done, 1)
                    if kind == "rope":
                        n, = a
                        dve.wait_ge(norm_done, it * NST + n + 1)
                        src = normed(n).rearrange("p (h d) -> p h d", d=D)
                        dst = roped(n).rearrange("p (h d) -> p h d", d=D)
                        for side, h0, h1 in ((0, 0, REP), (1, REP, REP + 1)):
                            last = dve.tensor_tensor(dst[:, h0:h1, :], src[:, h0:h1, :],
                                                     tabs[:, side, 0, n:n + 1, :].to_broadcast([P, h1 - h0, D]), ALU.mult)
                        last.then_inc(cosed, 1)
                        dve.wait_ge(cosed, it * NST + n + 1)
                        dve.wait_ge(rot_done, it * NST + n + 1)
                        dve.tensor_tensor(roped(n), roped(n), rotated(n), ALU.add).then_inc(rope_done, 1)
                    if kind == "turn":
                        n, = a
                        dve.wait_ge(qkhi_done, it * NST + n + 1)
                        dve.tensor_tensor(qk[:, 1, :, n * P:(n + 1) * P], pair(n), qk[:, 0, :, n * P:(n + 1) * P],
                                          ALU.subtract).then_inc(qklo_done, 1)
                    if kind == "S":
                        u, t = a
                        dve.wait_ge(s_done, it * UNITS * QT + u * QT + t + 1)
                        dve.tensor_reduce(nmax[:, u % 2, t:t + 1], s_ps[:, t % 2, 0:cols(t, u)], AX_X, ALU.max,
                                          negate=True).then_inc(max_done, 1)
                    if kind == "T":
                        u, j = a
                        k, c = blocks_before(u) + j, first_col(u, j)
                        dve.wait_ge(pthi_done, it * BLOCKS + k + 1)
                        dve.tensor_tensor(pT[:, k % PT_RING, 1, c:], t_ps[:, k % 2, c:], pT[:, k % PT_RING, 0, c:],
                                          ALU.subtract).then_inc(ptlo_done, 1)
                    if kind == "PV" and a[1] == blocks_of(a[0]) - 1:
                        u = a[0]
                        dve.wait_ge(ahi_done, it * UNITS + u + 1)
                        dve.tensor_tensor(aT[:, 1, u % REP, :], o_ps[:, u % 2, :], aT[:, 0, u % REP, :],
                                          ALU.subtract).then_inc(alo_done, 1)
                    if kind == "out":
                        i, = a
                        dve.wait_ge(out_done, 1 + it * NST + i + 1)
                        dve.tensor_tensor(yacc[:, i, :], yacc[:, i, :], o_ps[:, out_bank(i), :], ALU.add).then_inc(added, 1)

            with dve.Fori(0, B) as b:
                dve.wait_ge(yzero, b + 1)
                dve.tensor_copy(touched[:, 0:1], yacc[:, 0, 0:1])
                with dve.Fori(0, HKV) as kv:
                    body(b * HKV + kv)
                dve.wait_ge(added, 1 + (b + 1) * (HKV * NST))
                for t in range(NST):
                    dve.wait_ge(xg_in[t % 2], (b * (NST // 2) + t // 2 + 1) * 32)
                    dve.tensor_tensor(yacc[:, t, :], yacc[:, t, :], xg[:, t % 2, 1, :], ALU.mult).then_inc(mixed, 1)
                    dve.wait_ge(mixed, b * NST + t + 1)
                    dve.tensor_tensor(yacc[:, t, :], yacc[:, t, :], xg[:, t % 2, 0, :], ALU.add).then_inc(fin_done, 1)

        @block.tensor
        def _(pe):
            pe.sem_inc(qkv_done, 2)
            pe.sem_inc(out_done, 1)
            pe.wait_ge(consts_ready, 2)

            def body(it):
                for kind, *a in STEPS:
                    if kind == "qkv":
                        n, = a
                        if n == 0:
                            pe.wait_ge(w_in, (it + 1) * (16 * (REP + 2)))
                        pe.wait_ge(xt_in[n % 2], (it * (NST // 2) + n // 2 + 1) * 16)
                        if n >= 2:
                            pe.wait_ge(norm_done, it * NST + n - 1)
                            pe.wait_ge(vlo_done, it * NST + n - 1)
                        for k in range(KC):
                            for xp, wp in ((0, 0), (0, 1), (1, 0)):
                                lhs = xt[:, n % 2, xp, k, :]
                                first, final = k == 0 and xp == wp == 0, k == KC - 1 and xp == 1
                                pe.matmul(s_ps[:, n % 2, 0:REP * D], lhs, wT[:, wp, k, 0:REP * D], start=first, stop=final)
                                last = pe.matmul(s_ps[:, n % 2, REP * D:KV_COLS], lhs, wT[:, wp, k, REP * D:],
                                                 start=first, stop=final)
                        last.then_inc(qkv_done, 1)
                    if kind == "turn":
                        n, = a
                        pe.wait_ge(rope_done, it * NST + n + 1)
                        if n == 1:
                            pe.wait_ge(added, 1 + it * NST)
                        if n >= 2:
                            pe.wait_ge(qklo_done, it * NST + n - 1)
                        for h in range(REP + 1):
                            last = pe.transpose(pair(n)[:, h, :], roped(n)[:, h * D:(h + 1) * D], ident[:, :])
                        last.then_inc(turned, 1)
                    if kind == "S":
                        u, t = a
                        h, i = u % REP, QT * (u // REP) + t
                        k = it * UNITS * QT + u * QT + t
                        if u == 0 and t < 2:
                            pe.wait_ge(norm_done, it * NST + NST - 1 + t)
                            pe.wait_ge(vlo_done, it * NST + NST - 1 + t)
                        else:
                            pe.wait_ge(exp_done, k - 1)
                        if u == 0 and t == 0:
                            pe.wait_ge(qklo_done, it * NST + QT)
                        if u == REP and t == 0:
                            pe.wait_ge(qklo_done, it * NST + NST)
                        wide = -(-cols(t, u) // 256) * 256
                        for c0 in range(0, wide, 512):
                            c1 = min(wide, c0 + 512)
                            masked = c0 <= i * P < c1
                            for n, (qp, kp) in enumerate(((0, 0), (0, 1), (1, 0))):
                                last = pe.matmul(s_ps[:, t % 2, c0:c1], qk[:, qp, h, i * P:(i + 1) * P], qk[:, kp, REP, c0:c1],
                                                 start=n == 0, stop=n == 2 and not masked)
                            if masked:
                                last = pe.matmul(s_ps[:, t % 2, i * P:(i + 1) * P], identb[:, :], maskb[:, :],
                                                 start=False, stop=True)
                        last.then_inc(s_done, 1)
                    if kind == "T":
                        u, j = a
                        k = blocks_before(u) + j
                        if j == 0:
                            pe.wait_ge(p_done, it * UNITS * QT + (u + 1) * QT)
                        if k >= 2:
                            pe.wait_ge(ptlo_done, it * BLOCKS + k - 1)
                        else:
                            pe.wait_ge(qklo_done, it * NST + NST)
                        for t in range(first_col(u, j) // P, QT):
                            seen = j <= QT * (u // REP) + t
                            src = pbuf[:, u % 2, t, j * P:(j + 1) * P] if seen else zeros[:, :]
                            last = pe.transpose(t_ps[:, k % 2, t * P:(t + 1) * P], src, ident[:, :])
                        last.then_inc(pt_turned, 1)
                    if kind == "PV":
                        u, j = a
                        k, c = blocks_before(u) + j, first_col(u, j)
                        pe.wait_ge(ptlo_done, it * BLOCKS + k + 1)
                        if j == 0 and u >= 2:
                            if u == REP + 1:
                                pe.wait_ge(added, 1 + it * NST + QT)
                            pe.wait_ge(alo_done, it * UNITS + u - 1)
                        for n, (vp, pp) in enumerate(((0, 0), (0, 1), (1, 0))):
                            last = pe.matmul(o_ps[:, u % 2, c:], v[:, vp, j, :], pT[:, k % PT_RING, pp, c:],
                                             start=j == 0 and n == 0, stop=j == blocks_of(u) - 1 and n == 2)
                        if j == blocks_of(u) - 1:
                            last.then_inc(pv_done, 1)
                    if kind == "out":
                        i, = a
                        if i == 0:
                            pe.wait_ge(wo_in, (it + 1) * (16 * REP))
                            pe.wait_ge(alo_done, it * UNITS + REP)
                        elif i < QT:
                            pe.wait_ge(added, 1 + it * NST + i)
                        elif i == QT:
                            pe.wait_ge(alo_done, it * UNITS + UNITS)
                        elif i >= QT + 2:
                            pe.wait_ge(added, 1 + it * NST + i - 1)
                        t = i % QT
                        for h in range(REP):
                            for ap, wp in ((0, 0), (0, 1), (1, 0)):
                                last = pe.matmul(o_ps[:, out_bank(i), :], aT[:, ap, h, t * P:(t + 1) * P], woT[:, wp, h, :],
                                                 start=h == 0 and ap == wp == 0, stop=h == REP - 1 and ap == 1)
                        last.then_inc(out_done, 1)

            head_steps(pe, body)


INPUTS = {"x": "L0_attn_x", "wqkv": "L0_attn_w_qkv", "wo": "L0_attn_w_o", "wg": "L0_ffn_wq_gate",
          "wu": "L0_ffn_wq_up", "wd": "L0_ffn_wq_down", "sg": "L0_ffn_s_gate", "su": "L0_ffn_s_up",
          "sd": "L0_ffn_s_down"}


def build_program(nc, t, out):
    xT = nc.dram_tensor("xT_scratch", [TG, P, TPG, 2, KC, P], F32, kind="Internal").ap()
    wqkvT = nc.dram_tensor("wqkvT_scratch", [QKV_TILES, P, 2, KC, P], F32, kind="Internal").ap()
    woT = nc.dram_tensor("woT_scratch", [H, P, 2, KC, P], F32, kind="Internal").ap()
    gate = nc.dram_tensor("gate_scratch", [TILES, P, DIM], F32, kind="Internal").ap()
    x = t["x"].rearrange("b (t p) n -> (b t) p n", p=P)
    ffn_dram = {
        "x": x,
        "wqkv": t["wqkv"].rearrange("(r p) n -> r p n", p=P),
        "wo": t["wo"].rearrange("(r p) (h j) -> h p r j", p=P, j=P),
        "wg": t["wg"].rearrange("(c p) n -> c p n", p=P),
        "wu": t["wu"].rearrange("(c p) n -> c p n", p=P),
        "wd": t["wd"].rearrange("(r p) (c j) -> c p r j", p=P, j=P),
        "sg": t["sg"], "su": t["su"], "sd": t["sd"],
    }
    ffn_block(nc, ffn_dram, (xT, wqkvT, woT, gate))
    attention_block(nc, {"x": x, "cos": t["cos"], "ssin": t["ssin"], "norms": t["norms"], "norms_swapped": t["norms_swapped"]},
                    (xT, wqkvT, woT.rearrange("h p a c n -> h p a (c n)"), gate),
                    out.rearrange("b (t p) n -> (b t) p n", p=P))


def kernel(**inputs):
    import numpy as np
    from concourse import bacc
    from concourse.bass_utils import run_bass_kernel_spmd

    arrays = {short: np.ascontiguousarray(inputs[name]) for short, name in INPUTS.items()}
    norms = [np.asarray(inputs["L0_attn_" + n]) for n in ("qn_g", "qn_b", "kn_g", "kn_b")]
    arrays["norms"] = np.stack(norms)
    arrays["norms_swapped"] = np.stack([np.roll(n, D // 2) for n in norms])
    inv_freq = (1.0 / np.float32(1000000.0) ** (np.arange(0, D, 2, dtype=np.float32) / np.float32(D))).astype(np.float32)
    freqs = np.outer(np.arange(S, dtype=np.float32), inv_freq).astype(np.float32)
    cos, sin = np.cos(freqs.astype(np.float64)), np.sin(freqs.astype(np.float64))
    tiles = lambda a: np.ascontiguousarray(a.astype(np.float32).reshape(NST, P, D).transpose(1, 0, 2))
    arrays["cos"] = tiles(np.concatenate([cos, cos], 1))
    arrays["ssin"] = tiles(np.concatenate([-sin, sin], 1))

    nc = bacc.Bacc("TRN2", target_bir_lowering=False, num_devices=1)
    handles = {k: nc.dram_tensor(f"in_{k}", a.shape, mybir.dt.from_np(a.dtype), kind="ExternalInput").ap()
               for k, a in arrays.items()}
    out = nc.dram_tensor("out_x", (B, S, DIM), F32, kind="ExternalOutput").ap()
    build_program(nc, handles, out)
    r = run_bass_kernel_spmd(nc, [{f"in_{k}": a for k, a in arrays.items()}], core_ids=[0])
    return r.results[0]["out_x"]
```

```python
from contextlib import ExitStack

import concourse.bass as bass
from concourse import mybir

F32 = mybir.dt.float32
F32R = mybir.dt.float32r
BF16 = mybir.dt.bfloat16
I32 = mybir.dt.int32
ALU = mybir.AluOpType
ACT = mybir.ActivationFunctionType
AX_X = mybir.AxisListType.X

P = 128
B, S, DIM = 2, 1024, 512
H, HKV, D = 16, 4, 128
REP = H // HKV
HID = 1408
EPS = 1e-5
ZERO_POINT = 128.0
KC = DIM // P
NC = HID // P
TILES = B * S // P
TG = 4
TPG = TILES // TG
GTOK = TPG * P
QKV_TILES = (H + 2 * HKV)
NST = S // P
KV_COLS = (REP + 2) * D
QK_COLS = (REP + 1) * D


def ffn_events():
    first = [[] for _ in range(NC)]
    for c in range(NC - 1):
        first[c] = [("g", c + 1), ("u", c + 1), ("d", c + 1)]
    for t in range(TPG):
        first[2 + 2 * t].append(("x", t))
    for r in range(3):
        first[3 + 2 * r].append(("q", r))
    middle = [[] for _ in range(NC)]
    items = [("q", r) for r in range(7)] + [("o", h) for h in range(5)]
    for n, item in enumerate(items):
        middle[n * NC // len(items)].append(item)
    for t in range(TPG):
        middle[1 + 2 * t].append(("x", t))
    last = [[] for _ in range(NC)]
    items = [("q", r) for r in range(7)] + [("o", h) for h in range(6)]
    for n, item in enumerate(items):
        last[n * NC // len(items)].append(item)
    return first, middle, last


def ffn_block(nc, dram, scratch):
    x, wqkv, wo, wg, wu, wd, sg, su, sd = (
        dram[k] for k in ("x", "wqkv", "wo", "wg", "wu", "wd", "sg", "su", "sd"))
    xT_out, wqkvT_out, woT_out, gate_out = scratch
    FIRST, MIDDLE, LAST = ffn_events()
    prologue = [("x", t) for t in range(TPG)] + [("g", 0), ("u", 0), ("d", 0)]

    def slots(tg):
        return FIRST if isinstance(tg, int) and tg == 0 else LAST if isinstance(tg, int) and tg == TG - 1 else MIDDLE

    def flat(by_slot):
        return [e for slot in by_slot for e in slot]

    lists = {"pro": prologue, "first": flat(FIRST), "middle": flat(MIDDLE), "last": flat(LAST)}

    def count(events, kinds):
        return sum(e[0] in kinds for e in events)

    def before(tg, kinds):
        if isinstance(tg, int) and tg == 0:
            return count(prologue, kinds)
        return count(prologue, kinds) + count(lists["first"], kinds) + (tg - 1) * count(lists["middle"], kinds)

    RAW = "gudqo"
    STAGED = "qo"
    PRE = "gudx"
    RAW_RING, STAGE_RING, X_RING, H_RING, GU_RING = 2, 2, 2, 2, 3

    ctx = ExitStack()
    with ctx:
        def sb(name, shape, dt=F32):
            return ctx.enter_context(nc.sbuf_tensor(name, shape, dt))

        def sem(name):
            return ctx.enter_context(nc.semaphore(name))

        wgT = sb("wgT", [P, 2, KC, HID], F32R)
        wuT = sb("wuT", [P, 2, KC, HID], F32R)
        wdT = sb("wdT", [P, 2, NC, DIM], F32R)
        xT = sb("xT", [P, 2, TPG, 2, KC, P], F32R)
        hT = sb("hT", [P, H_RING, 2, GTOK], F32R)
        raw = sb("raw", [P, RAW_RING, DIM])
        stage = sb("stage", [P, STAGE_RING, 2, KC, P], F32R)
        xin = sb("xin", [P, X_RING, DIM])
        hf = sb("hf", [P, H_RING, GTOK])
        gbuf = sb("gbuf", [P, 2, DIM])
        sd_row = sb("sd_row", [P, DIM])
        s_col = sb("s_col", [P, 2, NC])
        ident = sb("ident", [P, P])
        stats = sb("stats", [P, X_RING, 6])
        moments = sb("moments", [P, X_RING, 2])
        veps = sb("veps", [P, X_RING, 1])
        rstd = sb("rstd", [P, X_RING, 1])
        minus_half = sb("minus_half", [P, 1])
        eps_col = sb("eps_col", [P, 1])
        touched = sb("touched", [P, 1])
        prep = ctx.enter_context(nc.psum_tensor("prep", [P, DIM], F32))
        gu = ctx.enter_context(nc.psum_tensor("gu", [P, GU_RING, GTOK], F32))
        y = ctx.enter_context(nc.psum_tensor("y", [P, TPG, DIM], F32))

        ident_zero = sem("ident_zero")
        ident_ready = sem("ident_ready")
        scales_in = sem("scales_in")
        raw_in = [sem(f"raw_in{i}") for i in range(RAW_RING)]
        x_in = [sem(f"x_in{i}") for i in range(X_RING)]
        stats_done = sem("stats_done")
        moments_done = sem("moments_done")
        veps_done = sem("veps_done")
        rstd_done = sem("rstd_done")
        pre_done = sem("pre_done")
        turned = sem("turned")
        hi_done = sem("hi_done")
        lo_done = sem("lo_done")
        stage_out = [sem(f"stage_out{i}") for i in range(STAGE_RING)]
        xT_stored = sem("xT_stored")
        gate_done = sem("gate_done")
        up_done = sem("up_done")
        silu_done = sem("silu_done")
        h_done = sem("h_done")
        hhi_done = sem("hhi_done")
        hlo_done = sem("hlo_done")
        down_done = sem("down_done")
        yscaled = sem("yscaled")
        g_done = sem("g_done")
        g_out = [sem(f"g_out{i}") for i in range(2)]

        def walk(tg):
            seen = []
            for c, events in enumerate(slots(tg)):
                for n, e in enumerate(events):
                    yield c, n, e, list(seen)
                    seen.append(e)

        def prologue_walk():
            for n, e in enumerate(prologue):
                yield 0, n, e, prologue[:n]

        def index(tg, seen, kinds="gudqox"):
            if tg is None:
                return count(seen, kinds)
            return before(tg, kinds) + count(seen, kinds)

        def ring(tg, seen, kinds, n):
            return count(seen, kinds) % n

        def uses(events, kinds, n, slot):
            return len(range(slot, count(events, kinds), n))

        def ring_uses(tg, seen, kinds, n, slot):
            within = uses(seen, kinds, n, slot)
            if tg is None:
                return within
            pro = uses(prologue, kinds, n, slot)
            if isinstance(tg, int) and tg == 0:
                return pro + within
            return (pro + uses(lists["first"], kinds, n, slot) + within
                    + (tg - 1) * uses(lists["middle"], kinds, n, slot))

        def previous(tg, seen, kinds, n):
            slot = ring(tg, seen, kinds, n)
            mine = [i for i, e in enumerate(seen) if e[0] in kinds]
            if len(mine) >= n:
                return (0 if tg is None else before(tg, "gudqox")) + mine[-n] + 1
            if tg is None:
                return None
            if isinstance(tg, int) and tg == 0:
                back, base = prologue, 0
            elif isinstance(tg, int) and tg == 1:
                back, base = lists["first"], before(0, "gudqox")
            else:
                return before(tg, "gudqox")
            mine = [i for i, e in enumerate(back) if e[0] in kinds]
            at = [i for k, i in enumerate(mine) if k % n == slot]
            return base + at[-1] + 1 if at else None

        def all_walks(engine, body):
            body(None)
            body(0)
            with engine.Fori(1, TG - 1) as tg:
                body(tg)
            body(TG - 1)

        block = ctx.enter_context(nc.Block())

        @block.gpsimd
        def _(pool):
            pool.memset(minus_half[:, :], -0.5).then_inc(ident_zero, 1)
            pool.memset(eps_col[:, :], EPS).then_inc(ident_zero, 1)
            pool.memset(ident[:, :], 0.0).then_inc(ident_zero, 1)
            pool.wait_ge(ident_zero, 3)
            pool.affine_select(out=ident[:, :], in_=ident[:, :], compare_op=ALU.not_equal, fill=1.0,
                               base=0, pattern=[[-1, P]], channel_multiplier=1).then_inc(ident_ready, 1)

            def rstd_of(n, slot):
                pool.wait_ge(moments_done, n + 1)
                pool.tensor_tensor(veps[:, slot, :], moments[:, slot, 1:2], eps_col[:, :], ALU.add).then_inc(veps_done, 1)
                pool.wait_ge(veps_done, n + 1)
                pool.tensor_tensor(rstd[:, slot, :], veps[:, slot, :], minus_half[:, :], ALU.pow).then_inc(rstd_done, 1)

            def low_of_h(n, s):
                pool.wait_ge(hhi_done, n + 1)
                pool.tensor_tensor(hT[:, s, 1, :], hf[:, s, :], hT[:, s, 0, :], ALU.subtract).then_inc(hlo_done, 1)

            def body(tg):
                events = prologue_walk() if tg is None else walk(tg)
                todo = {}
                for c, n, e, seen in events:
                    todo.setdefault(c, []).append((e, seen))
                for c in range(1 if tg is None else NC):
                    for e, seen in todo.get(c, []):
                        if e[0] == "x":
                            rstd_of(index(tg, seen, "x"), ring(tg, seen, "x", X_RING))
                    if tg is not None:
                        low_of_h(tg * NC + c, c % H_RING)

            all_walks(pool, body)

        @block.sync
        def _(sp):
            sp.dma_start(sd_row[:, :], sd.rearrange("(a n) -> a n", a=1).to_broadcast([P, DIM])).then_inc(scales_in, 16)
            with nc.allow_non_contiguous_dma(reason="two columns of scales, once"):
                sp.dma_start(s_col[:, 0, :], sg.rearrange("(c p) -> p c", p=P)).then_inc(scales_in, 16)
                sp.dma_start(s_col[:, 1, :], su.rearrange("(c p) -> p c", p=P)).then_inc(scales_in, 16)

            def load(tg, e, seen):
                kind, n = e
                prev = previous(tg, seen, "x" if kind == "x" else RAW, X_RING if kind == "x" else RAW_RING)
                if prev is not None:
                    sp.wait_ge(turned, prev)
                if kind == "x":
                    slot = ring(tg, seen, "x", X_RING)
                    tile = n if tg is None else (tg + 1) * TPG + n
                    sp.dma_start(xin[:, slot, :], x[tile]).then_inc(x_in[slot], 16)
                    return
                slot = ring(tg, seen, RAW, RAW_RING)
                done = 0 if tg is None or (isinstance(tg, int) and tg == 0) else before(tg, kind) if kind in "qo" else 0
                src = {"g": lambda: wg[n], "u": lambda: wu[n], "d": lambda: wd[n],
                       "q": lambda: wqkv[done + n], "o": lambda: wo[done + n]}[kind]()
                dst = raw[:, slot, :]
                if kind in "gud":
                    dst = dst.bitcast(I32)
                if kind in "do":
                    dst = dst.rearrange("p (r j) -> p r j", r=KC)
                sp.dma_start(dst, src).then_inc(raw_in[slot], 16)

            def store(tg, e, seen):
                kind, n = e
                if kind in STAGED:
                    slot = ring(tg, seen, STAGED, STAGE_RING)
                    done = 0 if isinstance(tg, int) and tg == 0 else before(tg, kind)
                    out = (wqkvT_out if kind == "q" else woT_out)[done + n]
                    sp.wait_ge(lo_done, index(tg, seen) + 1)
                    sp.dma_start(out, stage[:, slot].bitcast(F32)).then_inc(stage_out[slot], 16)
                if kind == "x" and n == TPG - 1:
                    group = 0 if tg is None else tg + 1
                    sp.wait_ge(lo_done, index(tg, seen) + 1)
                    sp.dma_start(xT_out[group], xT[:, group % 2].bitcast(F32)).then_inc(xT_stored, 16)

            def store_gate(tg, t):
                sp.wait_ge(g_done, tg * TPG + t + 1)
                sp.dma_start(gate_out[tg * TPG + t], gbuf[:, t % 2, :]).then_inc(g_out[t % 2], 16)

            def body(tg):
                events = [(c, e, seen) for c, _, e, seen in (prologue_walk() if tg is None else walk(tg))]
                for k in range(min(2, len(events))):
                    load(tg, *events[k][1:])
                at = 0
                for c in range(1 if tg is None else NC):
                    while at < len(events) and events[at][0] == c:
                        store(tg, *events[at][1:])
                        if at + 2 < len(events):
                            load(tg, *events[at + 2][1:])
                        at += 1
                    if c == 0 and tg is not None and not (isinstance(tg, int) and tg == 0):
                        for t in range(TPG):
                            store_gate(tg - 1, t)

            all_walks(sp, body)
            for t in range(TPG):
                store_gate(TG - 1, t)
            staged = lists["first"] + lists["middle"] * 2 + lists["last"]
            for slot in range(STAGE_RING):
                n = sum(uses(ev, STAGED, STAGE_RING, slot) * k
                        for ev, k in ((lists["first"], 1), (lists["middle"], TG - 2), (lists["last"], 1)))
                sp.wait_ge(stage_out[slot], 16 * n)
            sp.wait_ge(xT_stored, 16 * TG)
            for i in range(2):
                sp.wait_ge(g_out[i], 16 * TILES // 2)

        def destination(tg, e, seen, part):
            kind, n = e
            if kind == "x":
                parity = 0 if tg is None else (tg + 1) % 2
                return xT[:, parity, n, part]
            if kind in "gu":
                return (wgT if kind == "g" else wuT)[:, part, :, n * P:(n + 1) * P]
            if kind == "d":
                return wdT[:, part, n, :].rearrange("p (c n) -> p c n", c=KC)
            return stage[:, ring(tg, seen, STAGED, STAGE_RING), part]

        bank = prep[:, :].rearrange("p (c n) -> p c n", c=KC)

        @block.scalar
        def _(act):
            act.wait_ge(scales_in, 48)

            def high(tg, e, seen):
                i = index(tg, seen)
                kind, n = e
                if kind in STAGED:
                    slot = ring(tg, seen, STAGED, STAGE_RING)
                    used = ring_uses(tg, seen, STAGED, STAGE_RING, slot)
                    if not isinstance(used, int) or used > 0:
                        act.wait_ge(stage_out[slot], 16 * used)
                if kind == "x" and n == 0 and tg is not None:
                    if isinstance(tg, int) and tg == 0:
                        pass
                    else:
                        act.wait_ge(gate_done, tg * NC)
                        act.wait_ge(up_done, tg * NC)
                        act.wait_ge(xT_stored, 16 * tg)
                act.wait_ge(turned, i + 1)
                act.copy(destination(tg, e, seen, 0), bank).then_inc(hi_done, 1)

            def silu(tg, c):
                n = tg * NC + c
                act.wait_ge(gate_done, n + 1)
                if c >= H_RING:
                    act.wait_ge(hlo_done, n - H_RING + 1)
                elif not (isinstance(tg, int) and tg == 0):
                    act.wait_ge(hlo_done, tg * NC)
                act.activation(hf[:, c % H_RING, :], gu[:, (2 * c) % GU_RING, :], ACT.Silu,
                               scale=s_col[:, 0, c:c + 1]).then_inc(silu_done, 1)

            def high_of_h(tg, c):
                n = tg * NC + c
                act.wait_ge(h_done, n + 1)
                if c >= H_RING:
                    act.wait_ge(down_done, n - H_RING + 1)
                elif not (isinstance(tg, int) and tg == 0):
                    act.wait_ge(down_done, tg * NC - (1 - c) if c else tg * NC)
                act.copy(hT[:, c % H_RING, 0, :], hf[:, c % H_RING, :]).then_inc(hhi_done, 1)

            def gates(tg):
                for t in range(TPG):
                    act.wait_ge(yscaled, tg * TPG + t + 1)
                    act.activation(gbuf[:, t % 2, :], gbuf[:, t % 2, :], ACT.Silu).then_inc(g_done, 1)

            def body(tg):
                todo = {}
                for c, n, e, seen in (prologue_walk() if tg is None else walk(tg)):
                    todo.setdefault(c, []).append((e, seen))
                if tg is None:
                    for e, seen in todo[0]:
                        high(tg, e, seen)
                    return
                for c in range(NC):
                    events = todo.get(c, [])
                    for k, step in enumerate((lambda: silu(tg, c), lambda: high_of_h(tg, c), lambda: None, lambda: None)):
                        if k < len(events):
                            high(tg, *events[k])
                        step()
                    if c == 0 and not (isinstance(tg, int) and tg == 0):
                        gates(tg - 1)

            all_walks(act, body)
            gates(TG - 1)

        @block.vector
        def _(dve):
            def ready(tg, e, seen):
                kind, n = e
                if kind in "gud":
                    slot = ring(tg, seen, RAW, RAW_RING)
                    used = ring_uses(tg, seen, RAW, RAW_RING, slot)
                    dve.wait_ge(raw_in[slot], 16 * (used + 1))
                    dve.tensor_scalar(raw[:, slot, :], raw[:, slot, :].bitcast(I32), -ZERO_POINT, None,
                                      ALU.add).then_inc(pre_done, 1)
                if kind == "x":
                    slot = ring(tg, seen, "x", X_RING)
                    k = index(tg, seen, "x")
                    dve.wait_ge(x_in[slot], 16 * (ring_uses(tg, seen, "x", X_RING, slot) + 1))
                    dve.bn_stats(stats[:, slot, :], xin[:, slot, :]).then_inc(stats_done, 1)
                    dve.wait_ge(stats_done, k + 1)
                    dve.tensor_copy(touched[:, :], stats[:, slot, 0:1])
                    dve.bn_aggr(moments[:, slot, :], stats[:, slot, :]).then_inc(moments_done, 1)
                    dve.wait_ge(rstd_done, k + 1)
                    dve.tensor_scalar(xin[:, slot, :], xin[:, slot, :], moments[:, slot, 0:1], rstd[:, slot, :],
                                      ALU.subtract, ALU.mult).then_inc(pre_done, 1)

            def low(tg, e, seen):
                dve.wait_ge(hi_done, index(tg, seen) + 1)
                dve.tensor_tensor(destination(tg, e, seen, 1), bank, destination(tg, e, seen, 0),
                                  ALU.subtract).then_inc(lo_done, 1)

            def gated(tg, c):
                n = tg * NC + c
                dve.wait_ge(up_done, n + 1)
                dve.wait_ge(silu_done, n + 1)
                dve.scalar_tensor_tensor(hf[:, c % H_RING, :], gu[:, (2 * c + 1) % GU_RING, :], s_col[:, 1, c:c + 1],
                                         hf[:, c % H_RING, :], ALU.mult, ALU.mult).then_inc(h_done, 1)

            def scale_y(tg):
                dve.wait_ge(down_done, (tg + 1) * NC)
                for t in range(TPG):
                    if t >= 2 or not (isinstance(tg, int) and tg == 0):
                        dve.wait_ge(g_out[t % 2], 16 * (tg * (TPG // 2) + t // 2))
                    dve.tensor_tensor(gbuf[:, t % 2, :], y[:, t, :], sd_row[:, :], ALU.mult).then_inc(yscaled, 1)

            def body(tg):
                todo = {}
                events = [(c, e, seen) for c, _, e, seen in (prologue_walk() if tg is None else walk(tg))]
                for c, e, seen in events:
                    todo.setdefault(c, []).append((e, seen))
                following = [(e, seen) for _, e, seen in events][1:]
                if tg is None:
                    ready(tg, *todo[0][0])
                    for e, seen in todo[0]:
                        if following:
                            ready(tg, *following.pop(0))
                        low(tg, e, seen)
                    return
                ready(tg, *events[0][1:])
                for c in range(NC):
                    slot_events = todo.get(c, [])
                    for k in range(4):
                        if k < len(slot_events):
                            if following:
                                ready(tg, *following.pop(0))
                            low(tg, *slot_events[k])
                        if k == 1:
                            gated(tg, c)
                    if c == 0 and not (isinstance(tg, int) and tg == 0):
                        scale_y(tg - 1)

            dve.wait_ge(scales_in, 48)
            all_walks(dve, body)
            scale_y(TG - 1)

        @block.tensor
        def _(pe):
            pe.wait_ge(ident_ready, 1)

            def turn(tg, e, seen):
                kind, n = e
                if kind in PRE:
                    pe.wait_ge(pre_done, index(tg, seen, PRE) + 1)
                else:
                    slot = ring(tg, seen, RAW, RAW_RING)
                    pe.wait_ge(raw_in[slot], 16 * (ring_uses(tg, seen, RAW, RAW_RING, slot) + 1))
                i = index(tg, seen)
                if not (isinstance(i, int) and i == 0):
                    pe.wait_ge(lo_done, i)
                src = xin[:, ring(tg, seen, "x", X_RING), :] if kind == "x" else raw[:, ring(tg, seen, RAW, RAW_RING), :]
                for k in range(KC):
                    last = pe.transpose(prep[:, k * P:(k + 1) * P], src[:, k * P:(k + 1) * P], ident[:, :])
                last.then_inc(turned, 1)

            def hidden(tg, c, side):
                w = (wgT, wuT)[side]
                use = 2 * c + side
                if use >= GU_RING:
                    n = tg * NC + (use - GU_RING) // 2
                    pe.wait_ge(silu_done if (use - GU_RING) % 2 == 0 else h_done, n + 1)
                elif not (isinstance(tg, int) and tg == 0):
                    pe.wait_ge(silu_done, tg * NC)
                    pe.wait_ge(h_done, tg * NC)
                out = gu[:, use % GU_RING, :].rearrange("p (t n) -> p t n", t=TPG)
                parity = tg % 2
                for k in range(KC):
                    for wp, xp in ((0, 0), (0, 1), (1, 0)):
                        last = pe.matmul(out, w[:, wp, k, c * P:(c + 1) * P], xT[:, parity, :, xp, k, :],
                                         start=(k == 0 and wp == xp == 0), stop=(k == KC - 1 and wp == 1))
                last.then_inc(up_done if side else gate_done, 1)

            def down(tg, c):
                pe.wait_ge(hlo_done, tg * NC + c + 1)
                if c == 0 and not (isinstance(tg, int) and tg == 0):
                    pe.wait_ge(yscaled, tg * TPG)
                for t in range(TPG):
                    for hp, wp in ((0, 0), (0, 1), (1, 0)):
                        last = pe.matmul(y[:, t, :], hT[:, c % H_RING, hp, t * P:(t + 1) * P], wdT[:, wp, c, :],
                                         start=(c == 0 and hp == wp == 0), stop=(c == NC - 1 and hp == 1))
                last.then_inc(down_done, 1)

            def body(tg):
                todo = {}
                for c, n, e, seen in (prologue_walk() if tg is None else walk(tg)):
                    todo.setdefault(c, []).append((e, seen))
                if tg is None:
                    for e, seen in todo[0]:
                        turn(tg, e, seen)
                    pe.wait_ge(lo_done, len(prologue))
                    return
                for c in range(NC):
                    events = todo.get(c, [])
                    if c == 0:
                        pe.wait_ge(lo_done, before(tg, "gudqox"))
                    elif isinstance(tg, int) and tg == 0:
                        pe.wait_ge(lo_done, before(0, "gudqox") + sum(len(s) for s in FIRST[:c]))
                    steps = [lambda: hidden(tg, c, 0), lambda: hidden(tg, c, 1)]
                    if c > 0:
                        steps.append(lambda: down(tg, c - 1))
                    elif not (isinstance(tg, int) and tg == 0):
                        steps.append(lambda: down(tg - 1, NC - 1))
                    else:
                        steps.append(lambda: None)
                    for k, step in enumerate(steps):
                        if k < len(events):
                            turn(tg, *events[k])
                        step()
                    if len(events) > 3:
                        turn(tg, *events[3])

            all_walks(pe, body)
            down(TG - 1, NC - 1)


QT = 4
UNITS = 2 * REP
HALF = NST // 2
HEAD_RING = 4
LAG = 2
PT_RING = 3
MASKED = -3.0e38


def blocks_of(u):
    return QT * (u // REP + 1)


def blocks_before(u):
    return sum(blocks_of(v) for v in range(u))


BLOCKS = blocks_before(UNITS)

STAGES = (("qkv", 0), ("stats", 1), ("norm", 2), ("affine", 3), ("rope", 5), ("turn", 6))
ORDER = {kind: m for m, kind in enumerate(("turn", "rope", "norm", "affine", "stats", "qkv"))}
SECOND_AT, SECOND_GAP = 0, 2
FIRST_AT, FIRST_GAP = 17, 4
OUT_AT = (3, 4, 6, 7)


def token_tiles(tiles, at, gap):
    return [(at + gap * m + late, (kind, n)) for m, n in enumerate(tiles) for kind, late in STAGES]


def opening():
    placed = sorted(token_tiles(range(HALF), 0, 2), key=lambda p: (p[0], ORDER[p[1][0]]))
    return [step for _, step in placed] + [("spare_k",)] + [("S", 0, t) for t in range(QT)] + [("spare_v",)]


def maxima_first(steps):
    steps, at = list(steps), 0
    while at + 1 < len(steps):
        if steps[at][0][0] == "T" and steps[at + 1][0][0] == "S":
            steps[at], steps[at + 1] = steps[at + 1], steps[at]
        at += 1
    return steps


def schedule(another):
    beside = token_tiles(range(HALF, NST), SECOND_AT, SECOND_GAP)
    first = blocks_before(REP)
    if another:
        beside += token_tiles(range(HALF), FIRST_AT, FIRST_GAP)
    beside += [(first + late, ("out", t)) for t, late in enumerate(OUT_AT)]
    blocks = [(u, j) for u in range(UNITS) for j in range(blocks_of(u))]
    steps = []
    for k, (u, j) in enumerate(blocks):
        steps.append(("T", u, j))
        here = sorted((step for at, step in beside if at == k), key=lambda e: ORDER.get(e[0], 9))
        if another and (u, j) == (UNITS - 1, 0):
            steps.append(("spare_k",))
        if u + 1 < UNITS or another:
            where = (0, 0, 1, 1) if blocks_of(u) == QT else (0, 1, 2, 3)
            steps += [("S", (u + 1) % UNITS, t) for t in range(QT) if where[t] == j]
        steps += here
        if k >= LAG:
            steps.append(("PV", *blocks[k - LAG]))
            if another and blocks[k - LAG] == (UNITS - 1, HALF - 1):
                steps.append(("spare_v",))
    steps += [("PV", *e) for e in blocks[-LAG:]]
    steps += [("out", QT + t) for t in range(QT)]
    return steps


def attention_block(nc, dram, scratch, out):
    x, cos, ssin, norms = (dram[k] for k in ("x", "cos", "ssin", "norms"))
    xT_in, wqkvT_in, woT_in, gate_in = scratch
    HEADS = REP + 1
    ctx = ExitStack()
    with ctx:
        def sb(name, shape, dt=F32):
            return ctx.enter_context(nc.sbuf_tensor(name, shape, dt))

        def sem(name):
            return ctx.enter_context(nc.semaphore(name))

        wT = sb("wT", [P, 2, KC, KV_COLS], F32R)
        woT = sb("woT", [P, 2, REP, DIM], F32R)
        xt = sb("xt", [P, 2, 2, KC, P], F32R)
        qk = sb("qk", [P, 2, HEADS, S], F32R)
        v = sb("v", [P, 2, NST, D], F32R)
        k_spare = sb("k_spare", [P, 2, HALF * P], F32R)
        v_spare = sb("v_spare", [P, 2, HALF, D], F32R)
        pbuf = sb("pbuf", [P, 2, sum(QT + t + 1 for t in range(QT)) * P])
        pT = sb("pT", [P, PT_RING, 2, QT * P], F32R)
        aT = sb("aT", [P, 2, REP, QT * P], F32R)
        yacc = sb("yacc", [P, NST, DIM])
        cos_sb = sb("cos_sb", [P, NST, D // 2])
        ssin_sb = sb("ssin_sb", [P, NST, D])
        rows = sb("rows", [P, 2, HEADS, D])
        heads = sb("heads", [P, HEAD_RING, QK_COLS])
        rotated = sb("rotated", [P, QK_COLS])
        xg = sb("xg", [P, 2, 2, DIM])
        ident = sb("ident2", [P, P])
        identb = sb("identb", [P, P], BF16)
        maskb = sb("maskb", [P, P], BF16)
        zeros = sb("zeros", [P, P])
        stats = sb("stats2", [P, 2, HEADS, 6])
        moments = sb("moments2", [P, 2, HEADS, 2])
        veps = sb("veps2", [P, 2, HEADS])
        rstd = sb("rstd2", [P, 2, HEADS])
        nbias = sb("nbias", [P, 2, HEADS])
        minus_half = sb("minus_half2", [P, 1])
        minus_one = sb("minus_one", [P, 1])
        eps_col = sb("eps_col2", [P, 1])
        touched = sb("touched2", [P, 1])
        nmax = sb("nmax", [P, 2, QT])
        lsum = sb("lsum", [P, 2, QT])
        linv = sb("linv", [P, 2, QT])
        mask = pbuf[:, 1, 0:P]

        s_ps = ctx.enter_context(nc.psum_tensor("s_ps", [P, 2, S], F32))
        t_ps = ctx.enter_context(nc.psum_tensor("t_ps", [P, 2, QT * P], F32))
        o_ps = ctx.enter_context(nc.psum_tensor("o_ps", [P, 2, QT * P], F32))

        consts_made = sem("consts_made")
        consts_ready = sem("consts_ready")
        tables_in = sem("tables_in")
        rows_ready = sem("rows_ready")
        w_in = sem("w_in")
        wo_in = sem("wo_in")
        xt_in = [sem(f"xt_in{i}") for i in range(2)]
        qkv_done = sem("qkv_done")
        stats_done = sem("stats_done2")
        moments_done = sem("moments_done2")
        veps_done = sem("veps_done2")
        rstd_done = sem("rstd_done2")
        nbias_done = sem("nbias_done")
        norm_done = sem("norm_done")
        vhi_done = sem("vhi_done")
        vlo_done = sem("vlo_done")
        raw_done = sem("raw_done")
        scaled = sem("scaled")
        shifted = sem("shifted")
        affine_done = sem("affine_done")
        cosed = sem("cosed")
        rope_done = sem("rope_done")
        turned = sem("turned2")
        qkhi_done = sem("qkhi_done")
        qklo_done = sem("qklo_done")
        khi_moved = sem("khi_moved")
        klo_moved = sem("klo_moved")
        v_free = sem("v_free")
        vhi_moved = sem("vhi_moved")
        vlo_moved = sem("vlo_moved")
        s_done = sem("s_done")
        max_done = sem("max_done")
        exp_done = sem("exp_done")
        linv_done = sem("linv_done")
        p_done = sem("p_done")
        pt_turned = sem("pt_turned")
        pthi_done = sem("pthi_done")
        ptlo_done = sem("ptlo_done")
        pv_done = sem("pv_done")
        ahi_done = sem("ahi_done")
        alo_done = sem("alo_done")
        out_done = sem("out_done")
        added = sem("added")
        yzero = sem("yzero")
        xg_in = [sem(f"xg_in{i}") for i in range(2)]
        gated = sem("gated")
        fin_done = sem("fin_done")
        stored = [sem(f"stored{i}") for i in range(2)]

        def every_head(engine, body):
            body(-1, True, False)
            for b in range(B):
                with engine.Fori(b * HKV, (b + 1) * HKV - 1) as it:
                    body(it, True, False)
                body((b + 1) * HKV - 1, b + 1 < B, True)

        def steps_of(it, another):
            steps = opening() if isinstance(it, int) and it < 0 else schedule(another)
            held = [("S", 0, QT - 2), ("S", 0, QT - 1)]
            if isinstance(it, int) and it < 0:
                held = [None, None]
            at = 0
            for step in steps:
                slot = last = None
                if step[0] in ("S", "qkv", "turn"):
                    slot, last = at % 2, (held[at % 2], at < 2)
                    held[at % 2] = step
                    at += 1
                yield step, slot, last

        def tile_count(it, n):
            return HALF + it * NST + (n + HALF) % NST

        def s_count(it, u, t):
            return it * (UNITS * QT) + (u * QT + t if u else UNITS * QT + t)

        def cols(t, u):
            return (QT * (u // REP) + t + 1) * P

        def weights(u, t, c0, c1):
            at = sum(QT + s + 1 for s in range(t)) * P
            return pbuf[:, u % 2, at + c0:at + c1]

        def first_col(u, j):
            r = j - QT * (u // REP)
            return min(max(r, 0), 2) * P

        def out_bank(i):
            return 1 if i < QT else i % 2

        def k_place(n, part):
            if n < HALF:
                return k_spare[:, part, n * P:(n + 1) * P]
            return qk[:, part, REP, n * P:(n + 1) * P]

        def v_place(n, part):
            return v_spare[:, part, n, :] if n < HALF else v[:, part, n, :]

        def results_before(it):
            return (it // HKV) * NST

        block = ctx.enter_context(nc.Block())

        @block.sync
        def _(sp):
            def load_w(kv):
                for s, tile in enumerate([kv * REP + h for h in range(REP)] + [H + kv, H + HKV + kv]):
                    sp.dma_start(wT[:, :, :, s * D:(s + 1) * D].bitcast(F32), wqkvT_in[tile]).then_inc(w_in, 16)

            def load_x(it, b, n):
                k = tile_count(it, n)
                if not (isinstance(k, int) and k < 2):
                    sp.wait_ge(qkv_done, k - 1)
                sp.dma_start(xt[:, n % 2].bitcast(F32), xT_in[b * (TG // B) + n // TPG, :, n % TPG]).then_inc(xt_in[n % 2], 16)

            load_w(0)
            load_x(-1, 0, 0)
            load_x(-1, 0, 1)
            for part in range(2):
                for dst, src in ((rows[:, part, 0:REP, :], norms[part]), (rows[:, part, REP:HEADS, :], norms[2 + part])):
                    sp.dma_start(dst, src.rearrange("(o a d) -> o a d", o=1, a=1).to_broadcast([P, dst.shape[1], D])).then_inc(tables_in, 16)
            sp.dma_start(cos_sb[:, :, :], cos).then_inc(tables_in, 16)
            sp.dma_start(ssin_sb[:, :, :], ssin).then_inc(tables_in, 16)
            load_x(-1, 0, 2)
            load_x(-1, 0, 3)

            def head(it, b, another, final):
                kv = it - b * HKV
                load_x(it, b, HALF)
                load_x(it, b, HALF + 1)
                sp.wait_ge(out_done, 1 + it * NST)
                for h in range(REP):
                    sp.dma_start(woT[:, :, h, :].bitcast(F32), woT_in[kv * REP + h]).then_inc(wo_in, 16)
                load_x(it, b, HALF + 2)
                load_x(it, b, HALF + 3)
                if final:
                    load_result(it, 0)
                    load_result(it, 1)
                if another:
                    sp.wait_ge(qkv_done, tile_count(it, NST - 1) + 1)
                    load_w(0 if final else kv + 1)
                    for n in range(HALF):
                        load_x(it, b + 1 if final else b, n)
                if final:
                    for i in range(NST):
                        k = results_before(it) + i
                        sp.wait_ge(fin_done, k + 1)
                        sp.dma_start(out[k], xg[:, i % 2, 0, :]).then_inc(stored[i % 2], 16)
                        if i + 2 < NST:
                            load_result(it, i + 2)

            def load_result(it, i):
                k = results_before(it) + i
                if k >= 2:
                    sp.wait_ge(stored[i % 2], 16 * (k // 2))
                sp.dma_start(xg[:, i % 2, 0, :], x[k]).then_inc(xg_in[i % 2], 16)
                sp.dma_start(xg[:, i % 2, 1, :], gate_in[k]).then_inc(xg_in[i % 2], 16)

            for b in range(B):
                with sp.Fori(b * HKV, (b + 1) * HKV - 1) as it:
                    head(it, b, True, False)
                head((b + 1) * HKV - 1, b, b + 1 < B, True)
            for i in range(2):
                sp.wait_ge(stored[i], 16 * (B * NST // 2))

        @block.gpsimd
        def _(pool):
            pool.memset(ident[:, :], 0.0).then_inc(consts_made, 1)
            pool.memset(mask, 0.0).then_inc(consts_made, 1)
            pool.memset(zeros[:, :], 0.0).then_inc(consts_made, 1)
            pool.memset(minus_half[:, :], -0.5).then_inc(consts_made, 1)
            pool.memset(minus_one[:, :], -1.0).then_inc(consts_made, 1)
            pool.memset(eps_col[:, :], EPS).then_inc(consts_made, 1)
            pool.wait_ge(consts_made, 6)
            pool.affine_select(out=ident[:, :], in_=ident[:, :], compare_op=ALU.not_equal, fill=1.0,
                               base=0, pattern=[[-1, P]], channel_multiplier=1).then_inc(consts_made, 1)
            pool.affine_select(out=mask, in_=mask, compare_op=ALU.is_ge, fill=MASKED,
                               base=0, pattern=[[-1, P]], channel_multiplier=1).then_inc(consts_made, 1)
            pool.wait_ge(consts_made, 8)
            pool.tensor_copy(identb[:, :], ident[:, :]).then_inc(consts_ready, 1)
            pool.tensor_copy(maskb[:, :], mask).then_inc(consts_ready, 1)
            pool.memset(yacc[:, :, :], 0.0).then_inc(yzero, 1)
            pool.wait_ge(rows_ready, 2)

            def body(it, another, final):
                for (kind, *a), _, _ in steps_of(it, another):
                    if kind == "stats":
                        n, = a
                        k = tile_count(it, n)
                        pool.wait_ge(moments_done, k + 1)
                        if not (isinstance(k, int) and k < 2):
                            pool.wait_ge(norm_done, k - 1)
                        pool.tensor_tensor(veps[:, n % 2, :], moments[:, n % 2, :, 1],
                                           eps_col[:, :].to_broadcast([P, HEADS]), ALU.add).then_inc(veps_done, 1)
                        pool.wait_ge(veps_done, k + 1)
                        pool.tensor_tensor(rstd[:, n % 2, :], veps[:, n % 2, :],
                                           minus_half[:, :].to_broadcast([P, HEADS]), ALU.pow).then_inc(rstd_done, 1)
                    if kind == "affine":
                        n, = a
                        k = tile_count(it, n)
                        y = heads[:, n % HEAD_RING, :].rearrange("p (h d) -> p h d", d=D)
                        pool.wait_ge(scaled, k + 1)
                        pool.tensor_tensor(y, y, rows[:, 1], ALU.add).then_inc(shifted, 1)
                        pool.wait_ge(shifted, k + 1)
                        if not (isinstance(k, int) and k < 1):
                            pool.wait_ge(rope_done, k)
                        y = heads[:, n % HEAD_RING, :].rearrange("p (h s d) -> p h s d", s=2, d=D // 2)
                        r = rotated[:, :].rearrange("p (h s d) -> p h s d", s=2, d=D // 2)
                        for s in range(2):
                            sine = ssin_sb[:, n:n + 1, s * (D // 2):(s + 1) * (D // 2)].to_broadcast([P, HEADS, D // 2])
                            last = pool.tensor_tensor(r[:, :, s, :], y[:, :, 1 - s, :], sine, ALU.mult)
                        last.then_inc(affine_done, 1)
                    if kind == "S":
                        u, t = a
                        k = s_count(it, u, t)
                        pool.wait_ge(exp_done, k + 1)
                        pool.tensor_tensor(linv[:, u % 2, t:t + 1], lsum[:, u % 2, t:t + 1], minus_one[:, :],
                                           ALU.pow).then_inc(linv_done, 1)
                        pool.wait_ge(linv_done, k + 1)
                        w = weights(u, t, 0, cols(t, u))
                        pool.tensor_tensor(w, w, linv[:, u % 2, t:t + 1].to_broadcast([P, cols(t, u)]),
                                           ALU.mult).then_inc(p_done, 1)

            every_head(pool, body)

        @block.scalar
        def _(act):
            def body(it, another, final):
                for (kind, *a), slot, _ in steps_of(it, another):
                    if kind == "qkv":
                        n, = a
                        k = tile_count(it, n)
                        act.wait_ge(qkv_done, k + 1)
                        act.copy(v_place(n, 0), s_ps[:, slot, QK_COLS:KV_COLS]).then_inc(vhi_done, 1)
                        if not (isinstance(k, int) and k < HEAD_RING):
                            act.wait_ge(turned, k - HEAD_RING + 1)
                        act.copy(heads[:, n % HEAD_RING, :], s_ps[:, slot, 0:QK_COLS]).then_inc(raw_done, 1)
                    if kind == "norm":
                        n, = a
                        k = tile_count(it, n)
                        act.wait_ge(nbias_done, k + 1)
                        for h in range(HEADS):
                            y = heads[:, n % HEAD_RING, h * D:(h + 1) * D]
                            last = act.activation(y, y, ACT.Identity, bias=nbias[:, n % 2, h:h + 1], scale=rstd[:, n % 2, h:h + 1])
                        last.then_inc(norm_done, 1)
                    if kind == "turn":
                        n, = a
                        act.wait_ge(turned, tile_count(it, n) + 1)
                        src = s_ps[:, slot, 0:QK_COLS].rearrange("p (h t) -> p h t", t=P)
                        act.copy(qk[:, 0, 0:REP, n * P:(n + 1) * P], src[:, 0:REP, :])
                        act.copy(k_place(n, 0), src[:, REP, :]).then_inc(qkhi_done, 1)
                    if kind == "spare_k":
                        act.wait_ge(qkhi_done, tile_count(it, HALF - 1) + 1)
                        if not (isinstance(it, int) and it < 0):
                            act.wait_ge(s_done, s_count(it, UNITS - 1, QT - 1) + 1)
                        act.copy(qk[:, 0, REP, 0:HALF * P], k_spare[:, 0, :]).then_inc(khi_moved, 1)
                    if kind == "spare_v":
                        act.wait_ge(vhi_done, tile_count(it, HALF - 1) + 1)
                        if not (isinstance(it, int) and it < 0):
                            act.wait_ge(v_free, it + 1)
                        act.copy(v[:, 0, 0:HALF, :], v_spare[:, 0]).then_inc(vhi_moved, 1)
                    if kind == "S":
                        u, t = a
                        act.wait_ge(max_done, s_count(it, u, t) + 1)
                        act.activation(weights(u, t, 0, cols(t, u)), s_ps[:, slot, 0:cols(t, u)], ACT.Exp,
                                       bias=nmax[:, u % 2, t:t + 1], scale=1.0,
                                       accum_out=lsum[:, u % 2, t:t + 1]).then_inc(exp_done, 1)
                    if kind == "T":
                        u, j = a
                        k, c = blocks_before(u) + j, first_col(u, j)
                        act.wait_ge(pt_turned, it * BLOCKS + k + 1)
                        act.copy(pT[:, k % PT_RING, 0, c:], t_ps[:, k % 2, c:]).then_inc(pthi_done, 1)
                    if kind == "PV" and a[1] == blocks_of(a[0]) - 1:
                        u = a[0]
                        act.wait_ge(pv_done, it * UNITS + u + 1)
                        act.copy(aT[:, 0, u % REP, :], o_ps[:, u % 2, :]).then_inc(ahi_done, 1)

            act.wait_ge(consts_ready, 2)
            every_head(act, body)

        @block.vector
        def _(dve):
            dve.sem_inc(added, 1)
            dve.wait_ge(tables_in, 96)
            for part in range(2):
                dve.tensor_scalar(rows[:, part, 0:REP, :], rows[:, part, 0:REP, :], D ** -0.5, None,
                                  ALU.mult).then_inc(rows_ready, 1)
            dve.wait_ge(yzero, 1)

            def body(it, another, final):
                for (kind, *a), slot, _ in maxima_first(steps_of(it, another)):
                    if kind == "qkv":
                        n, = a
                        k = tile_count(it, n)
                        dve.wait_ge(vhi_done, k + 1)
                        dve.wait_ge(raw_done, k + 1)
                        dve.tensor_tensor(v_place(n, 1), s_ps[:, slot, QK_COLS:KV_COLS], v_place(n, 0),
                                          ALU.subtract).then_inc(vlo_done, 1)
                    if kind == "stats":
                        n, = a
                        k = tile_count(it, n)
                        for h in range(HEADS):
                            last = dve.bn_stats(stats[:, n % 2, h, :], heads[:, n % HEAD_RING, h * D:(h + 1) * D])
                        last.then_inc(stats_done, 1)
                        dve.wait_ge(stats_done, k + 1)
                        dve.tensor_copy(touched[:, :], stats[:, n % 2, HEADS - 1, 0:1])
                        for h in range(HEADS):
                            last = dve.bn_aggr(moments[:, n % 2, h, :], stats[:, n % 2, h, :])
                        last.then_inc(moments_done, 1)
                    if kind == "norm":
                        n, = a
                        k = tile_count(it, n)
                        dve.wait_ge(rstd_done, k + 1)
                        if not (isinstance(k, int) and k < 2):
                            dve.wait_ge(norm_done, k - 1)
                        dve.scalar_tensor_tensor(nbias[:, n % 2, :], moments[:, n % 2, :, 0], -1.0, rstd[:, n % 2, :],
                                                 ALU.mult, ALU.mult).then_inc(nbias_done, 1)
                    if kind == "affine":
                        n, = a
                        y = heads[:, n % HEAD_RING, :].rearrange("p (h d) -> p h d", d=D)
                        dve.wait_ge(norm_done, tile_count(it, n) + 1)
                        dve.tensor_tensor(y, y, rows[:, 0], ALU.mult).then_inc(scaled, 1)
                    if kind == "rope":
                        n, = a
                        k = tile_count(it, n)
                        y = heads[:, n % HEAD_RING, :]
                        dve.wait_ge(affine_done, k + 1)
                        dve.tensor_tensor(y.rearrange("p (h d) -> p h d", d=D // 2), y.rearrange("p (h d) -> p h d", d=D // 2),
                                          cos_sb[:, n:n + 1, :].to_broadcast([P, 2 * HEADS, D // 2]), ALU.mult).then_inc(cosed, 1)
                        dve.wait_ge(cosed, k + 1)
                        dve.tensor_tensor(y, y, rotated[:, :], ALU.add).then_inc(rope_done, 1)
                    if kind == "turn":
                        n, = a
                        dve.wait_ge(qkhi_done, tile_count(it, n) + 1)
                        src = s_ps[:, slot, 0:QK_COLS].rearrange("p (h t) -> p h t", t=P)
                        here = qk[:, :, 0:REP, n * P:(n + 1) * P]
                        dve.tensor_tensor(here[:, 1], src[:, 0:REP, :], here[:, 0], ALU.subtract)
                        dve.tensor_tensor(k_place(n, 1), src[:, REP, :], k_place(n, 0), ALU.subtract).then_inc(qklo_done, 1)
                    if kind == "spare_k":
                        dve.wait_ge(qklo_done, tile_count(it, HALF - 1) + 1)
                        if not (isinstance(it, int) and it < 0):
                            dve.wait_ge(s_done, s_count(it, UNITS - 1, QT - 1) + 1)
                        dve.tensor_copy(qk[:, 1, REP, 0:HALF * P], k_spare[:, 1, :]).then_inc(klo_moved, 1)
                    if kind == "spare_v":
                        dve.wait_ge(vlo_done, tile_count(it, HALF - 1) + 1)
                        if not (isinstance(it, int) and it < 0):
                            dve.wait_ge(v_free, it + 1)
                        dve.tensor_copy(v[:, 1, 0:HALF, :], v_spare[:, 1]).then_inc(vlo_moved, 1)
                    if kind == "S":
                        u, t = a
                        dve.wait_ge(s_done, s_count(it, u, t) + 1)
                        dve.tensor_reduce(nmax[:, u % 2, t:t + 1], s_ps[:, slot, 0:cols(t, u)], AX_X, ALU.max,
                                          negate=True).then_inc(max_done, 1)
                    if kind == "T":
                        u, j = a
                        k, c = blocks_before(u) + j, first_col(u, j)
                        dve.wait_ge(pthi_done, it * BLOCKS + k + 1)
                        dve.tensor_tensor(pT[:, k % PT_RING, 1, c:], t_ps[:, k % 2, c:], pT[:, k % PT_RING, 0, c:],
                                          ALU.subtract).then_inc(ptlo_done, 1)
                    if kind == "PV" and a[1] == blocks_of(a[0]) - 1:
                        u = a[0]
                        dve.wait_ge(ahi_done, it * UNITS + u + 1)
                        dve.tensor_tensor(aT[:, 1, u % REP, :], o_ps[:, u % 2, :], aT[:, 0, u % REP, :],
                                          ALU.subtract).then_inc(alo_done, 1)
                    if kind == "out":
                        i, = a
                        dve.wait_ge(out_done, 1 + it * NST + i + 1)
                        dve.tensor_tensor(yacc[:, i, :], yacc[:, i, :], o_ps[:, out_bank(i), :], ALU.add).then_inc(added, 1)
                        if final:
                            k = results_before(it) + i
                            dve.wait_ge(added, 1 + it * NST + i + 1)
                            dve.wait_ge(xg_in[i % 2], 32 * (k // 2 + 1))
                            dve.tensor_tensor(yacc[:, i, :], yacc[:, i, :], xg[:, i % 2, 1, :], ALU.mult).then_inc(gated, 1)
                            dve.wait_ge(gated, k + 1)
                            dve.tensor_tensor(xg[:, i % 2, 0, :], yacc[:, i, :], xg[:, i % 2, 0, :], ALU.add).then_inc(fin_done, 1)
                            if another:
                                dve.wait_ge(fin_done, k + 1)
                                dve.memset(yacc[:, i, :], 0.0)

            every_head(dve, body)

        @block.tensor
        def _(pe):
            pe.sem_inc(out_done, 1)
            pe.wait_ge(consts_ready, 2)

            def wait_for_slot(it, last):
                step, earlier = last
                if step is None:
                    return
                kind, *a = step
                it = it - 1 if earlier else it
                if kind == "S":
                    pe.wait_ge(exp_done, s_count(it, *a) + 1)
                if kind == "qkv":
                    pe.wait_ge(vlo_done, tile_count(it, *a) + 1)
                if kind == "turn":
                    pe.wait_ge(qklo_done, tile_count(it, *a) + 1)

            def body(it, another, final):
                for (kind, *a), slot, last_use in steps_of(it, another):
                    if slot is not None:
                        wait_for_slot(it, last_use)
                    if kind == "qkv":
                        n, = a
                        k = tile_count(it, n)
                        if n == 0:
                            pe.wait_ge(w_in, (it + 2) * (16 * (REP + 2)))
                        pe.wait_ge(xt_in[n % 2], (it * (NST // 2) + HALF // 2 + ((n + HALF) % NST) // 2 + 1) * 16)
                        for c in range(KC):
                            for xp, wp in ((0, 0), (0, 1), (1, 0)):
                                lhs = xt[:, n % 2, xp, c, :]
                                first, final_one = c == 0 and xp == wp == 0, c == KC - 1 and xp == 1
                                pe.matmul(s_ps[:, slot, 0:REP * D], lhs, wT[:, wp, c, 0:REP * D], start=first, stop=final_one)
                                last = pe.matmul(s_ps[:, slot, REP * D:KV_COLS], lhs, wT[:, wp, c, REP * D:],
                                                 start=first, stop=final_one)
                        last.then_inc(qkv_done, 1)
                    if kind == "turn":
                        n, = a
                        pe.wait_ge(rope_done, tile_count(it, n) + 1)
                        for h in range(HEADS):
                            last = pe.transpose(s_ps[:, slot, h * P:(h + 1) * P], heads[:, n % HEAD_RING, h * D:(h + 1) * D], ident[:, :])
                        last.then_inc(turned, 1)
                    if kind == "S":
                        u, t = a
                        h, i = u % REP, QT * (u // REP) + t
                        if u == 0 and t == 0:
                            pe.wait_ge(qklo_done, tile_count(it, HALF - 1) + 1)
                            pe.wait_ge(khi_moved, it + 2)
                            pe.wait_ge(klo_moved, it + 2)
                        if u == REP:
                            pe.wait_ge(qklo_done, tile_count(it, HALF + (t | 1)) + 1)
                        wide = -(-cols(t, u) // 256) * 256
                        for c0 in range(0, wide, 512):
                            c1 = min(wide, c0 + 512)
                            masked = c0 <= i * P < c1
                            for n, (qp, kp) in enumerate(((0, 0), (0, 1), (1, 0))):
                                last = pe.matmul(s_ps[:, slot, c0:c1], qk[:, qp, h, i * P:(i + 1) * P], qk[:, kp, REP, c0:c1],
                                                 start=n == 0, stop=n == 2 and not masked)
                            if masked:
                                last = pe.matmul(s_ps[:, slot, i * P:(i + 1) * P], identb[:, :], maskb[:, :],
                                                 start=False, stop=True)
                        last.then_inc(s_done, 1)
                    if kind == "T":
                        u, j = a
                        k = blocks_before(u) + j
                        if j == 0:
                            pe.wait_ge(p_done, it * UNITS * QT + (u + 1) * QT)
                        if k >= 2:
                            pe.wait_ge(ptlo_done, it * BLOCKS + k - 1)
                        for t in range(first_col(u, j) // P, QT):
                            seen = j <= QT * (u // REP) + t
                            src = weights(u, t, j * P, (j + 1) * P) if seen else zeros[:, :]
                            last = pe.transpose(t_ps[:, k % 2, t * P:(t + 1) * P], src, ident[:, :])
                        last.then_inc(pt_turned, 1)
                    if kind == "PV":
                        u, j = a
                        k, c = blocks_before(u) + j, first_col(u, j)
                        pe.wait_ge(ptlo_done, it * BLOCKS + k + 1)
                        if j == 0:
                            if u == 0:
                                pe.wait_ge(added, 1 + it * NST)
                                pe.wait_ge(vhi_moved, it + 1)
                                pe.wait_ge(vlo_moved, it + 1)
                            if u == REP + 1:
                                pe.wait_ge(added, 1 + it * NST + QT)
                            if u >= 2:
                                pe.wait_ge(alo_done, it * UNITS + u - 1)
                        for n, (vp, pp) in enumerate(((0, 0), (0, 1), (1, 0))):
                            last = pe.matmul(o_ps[:, u % 2, c:], v[:, vp, j, :], pT[:, k % PT_RING, pp, c:],
                                             start=j == 0 and n == 0, stop=j == blocks_of(u) - 1 and n == 2)
                        if j == blocks_of(u) - 1:
                            last.then_inc(pv_done, 1)
                        elif (u, j) == (UNITS - 1, HALF - 1):
                            last.then_inc(v_free, 1)
                    if kind == "out":
                        i, = a
                        if i == 0:
                            pe.wait_ge(wo_in, (it + 1) * (16 * REP))
                            pe.wait_ge(alo_done, it * UNITS + REP)
                        elif i < QT:
                            pe.wait_ge(added, 1 + it * NST + i)
                        elif i == QT:
                            pe.wait_ge(alo_done, it * UNITS + UNITS)
                        elif i >= QT + 2:
                            pe.wait_ge(added, 1 + it * NST + i - 1)
                        t = i % QT
                        for h in range(REP):
                            for ap, wp in ((0, 0), (0, 1), (1, 0)):
                                last = pe.matmul(o_ps[:, out_bank(i), :], aT[:, ap, h, t * P:(t + 1) * P], woT[:, wp, h, :],
                                                 start=h == 0 and ap == wp == 0, stop=h == REP - 1 and ap == 1)
                        last.then_inc(out_done, 1)

            every_head(pe, body)


INPUTS = {"x": "L0_attn_x", "wqkv": "L0_attn_w_qkv", "wo": "L0_attn_w_o", "wg": "L0_ffn_wq_gate",
          "wu": "L0_ffn_wq_up", "wd": "L0_ffn_wq_down", "sg": "L0_ffn_s_gate", "su": "L0_ffn_s_up",
          "sd": "L0_ffn_s_down", "qg": "L0_attn_qn_g", "qb": "L0_attn_qn_b", "kg": "L0_attn_kn_g", "kb": "L0_attn_kn_b"}
NORMS = ("qg", "qb", "kg", "kb")


def build_program(nc, t, out):
    xT = nc.dram_tensor("xT_scratch", [TG, P, TPG, 2, KC, P], F32, kind="Internal").ap()
    wqkvT = nc.dram_tensor("wqkvT_scratch", [QKV_TILES, P, 2, KC, P], F32, kind="Internal").ap()
    woT = nc.dram_tensor("woT_scratch", [H, P, 2, KC, P], F32, kind="Internal").ap()
    gate = nc.dram_tensor("gate_scratch", [TILES, P, DIM], F32, kind="Internal").ap()
    x = t["x"].rearrange("b (t p) n -> (b t) p n", p=P)
    ffn_dram = {
        "x": x,
        "wqkv": t["wqkv"].rearrange("(r p) n -> r p n", p=P),
        "wo": t["wo"].rearrange("(r p) (h j) -> h p r j", p=P, j=P),
        "wg": t["wg"].rearrange("(c p) n -> c p n", p=P),
        "wu": t["wu"].rearrange("(c p) n -> c p n", p=P),
        "wd": t["wd"].rearrange("(r p) (c j) -> c p r j", p=P, j=P),
        "sg": t["sg"], "su": t["su"], "sd": t["sd"],
    }
    ffn_block(nc, ffn_dram, (xT, wqkvT, woT, gate))
    attention_block(nc, {"x": x, "cos": t["cos"], "ssin": t["ssin"], "norms": [t[n] for n in NORMS]},
                    (xT, wqkvT, woT.rearrange("h p a c n -> h p a (c n)"), gate),
                    out.rearrange("b (t p) n -> (b t) p n", p=P))


def kernel(**inputs):
    import numpy as np
    from concourse import bacc
    from concourse.bass_utils import run_bass_kernel_spmd

    arrays = {short: np.ascontiguousarray(inputs[name]) for short, name in INPUTS.items()}
    inv_freq = (1.0 / np.float32(1000000.0) ** (np.arange(0, D, 2, dtype=np.float32) / np.float32(D))).astype(np.float32)
    freqs = np.outer(np.arange(S, dtype=np.float32), inv_freq).astype(np.float32)
    cos, sin = np.cos(freqs.astype(np.float64)), np.sin(freqs.astype(np.float64))
    tiles = lambda a: np.ascontiguousarray(a.astype(np.float32).reshape(NST, P, -1).transpose(1, 0, 2))
    arrays["cos"] = tiles(cos)
    arrays["ssin"] = tiles(np.concatenate([-sin, sin], 1))

    nc = bacc.Bacc("TRN2", target_bir_lowering=False, num_devices=1)
    handles = {k: nc.dram_tensor(f"in_{k}", a.shape, mybir.dt.from_np(a.dtype), kind="ExternalInput").ap()
               for k, a in arrays.items()}
    out = nc.dram_tensor("out_x", (B, S, DIM), F32, kind="ExternalOutput").ap()
    build_program(nc, handles, out)
    r = run_bass_kernel_spmd(nc, [{f"in_{k}": a for k, a in arrays.items()}], core_ids=[0])
    return r.results[0]["out_x"]
```

```python
from contextlib import ExitStack

import concourse.bass as bass
from concourse import mybir

F32 = mybir.dt.float32
F32R = mybir.dt.float32r
BF16 = mybir.dt.bfloat16
I32 = mybir.dt.int32
ALU = mybir.AluOpType
ACT = mybir.ActivationFunctionType
AX_X = mybir.AxisListType.X

P = 128
B, S, DIM = 2, 1024, 512
H, HKV, D = 16, 4, 128
REP = H // HKV
HID = 1408
EPS = 1e-5
ZERO_POINT = 128.0
KC = DIM // P
NC = HID // P
TILES = B * S // P
TG = 4
TPG = TILES // TG
GTOK = TPG * P
QKV_TILES = (H + 2 * HKV)
NST = S // P
KV_COLS = (REP + 2) * D
QK_COLS = (REP + 1) * D


def ffn_events():
    first = [[("d", c)] + [("g", c + 1), ("u", c + 1)] * (c < NC - 1) for c in range(NC)]
    for t in range(TPG):
        first[min(3 + 3 * t, NC - 1)].append(("x", t))
    middle = [[] for _ in range(NC)]
    items = [("q", r) for r in range(8)] + [("o", h) for h in range(5)]
    for n, item in enumerate(items):
        middle[1 + n * (NC - 1) // len(items)].append(item)
    for t in range(TPG):
        middle[1 + 2 * t].append(("x", t))
    last = [[] for _ in range(NC)]
    items = [("q", r) for r in range(8)] + [("o", h) for h in range(6)]
    for n, item in enumerate(items):
        last[1 + n * (NC - 1) // len(items)].append(item)
    return first, middle, last


def ffn_block(nc, dram, scratch):
    x, wqkv, wo, wg, wu, wd, sg, su, sd = (
        dram[k] for k in ("x", "wqkv", "wo", "wg", "wu", "wd", "sg", "su", "sd"))
    xT_out, wqkvT_out, woT_out, gate_out = scratch
    FIRST, MIDDLE, LAST = ffn_events()
    prologue = [("x", 0), ("g", 0), ("x", 1), ("u", 0), ("x", 2), ("x", 3)]

    def slots(tg):
        return FIRST if isinstance(tg, int) and tg == 0 else LAST if isinstance(tg, int) and tg == TG - 1 else MIDDLE

    def flat(by_slot):
        return [e for slot in by_slot for e in slot]

    lists = {"pro": prologue, "first": flat(FIRST), "middle": flat(MIDDLE), "last": flat(LAST)}

    def count(events, kinds):
        return sum(e[0] in kinds for e in events)

    def before(tg, kinds):
        if isinstance(tg, int) and tg == 0:
            return count(prologue, kinds)
        return count(prologue, kinds) + count(lists["first"], kinds) + (tg - 1) * count(lists["middle"], kinds)

    RAW = "gudqo"
    STAGED = "qo"
    PRE = "gudx"
    RAW_RING, STAGE_RING, X_RING, H_RING, GU_RING = 4, 2, 2, 2, 3
    AHEAD = 4

    ctx = ExitStack()
    with ctx:
        def sb(name, shape, dt=F32):
            return ctx.enter_context(nc.sbuf_tensor(name, shape, dt))

        def sem(name):
            return ctx.enter_context(nc.semaphore(name))

        wgT = sb("wgT", [P, 2, KC, HID], F32R)
        wuT = sb("wuT", [P, 2, KC, HID], F32R)
        wdT = sb("wdT", [P, 2, NC, DIM], F32R)
        xT = sb("xT", [P, 2, TPG, 2, KC, P], F32R)
        hT = sb("hT", [P, H_RING, 2, GTOK], F32R)
        raw = sb("raw", [P, RAW_RING, DIM])
        stage = sb("stage", [P, STAGE_RING, 2, KC, P], F32R)
        xin = sb("xin", [P, X_RING, DIM])
        hf = sb("hf", [P, H_RING, GTOK])
        gbuf = sb("gbuf", [P, TPG, DIM])
        sd_row = sb("sd_row", [P, DIM])
        s_col = sb("s_col", [P, 2, NC])
        ident = sb("ident", [P, P])
        stats = sb("stats", [P, X_RING, 6])
        moments = sb("moments", [P, X_RING, 2])
        veps = sb("veps", [P, X_RING, 1])
        rstd = sb("rstd", [P, X_RING, 1])
        minus_half = sb("minus_half", [P, 1])
        eps_col = sb("eps_col", [P, 1])
        touched = sb("touched", [P, 1])
        ones = sb("ones", [P, P])
        any_low = sb("any_low", [P, 1])
        wide = sb("wide", [P, 1], I32)
        low_bits = gbuf[:, 1, :].bitcast(I32)
        prep = ctx.enter_context(nc.psum_tensor("prep", [P, DIM], F32))
        gu = ctx.enter_context(nc.psum_tensor("gu", [P, GU_RING, GTOK], F32))
        y = ctx.enter_context(nc.psum_tensor("y", [P, TPG, DIM], F32))

        ident_zero = sem("ident_zero")
        ident_ready = sem("ident_ready")
        ones_ready = sem("ones_ready")
        bits_done = sem("bits_done")
        any_low_done = sem("any_low_done")
        counted = sem("counted")
        wide_done = sem("wide_done")
        scales_in = sem("scales_in")
        raw_in = [sem(f"raw_in{i}") for i in range(RAW_RING)]
        x_in = [sem(f"x_in{i}") for i in range(X_RING)]
        stats_done = sem("stats_done")
        moments_done = sem("moments_done")
        veps_done = sem("veps_done")
        rstd_done = sem("rstd_done")
        pre_done = sem("pre_done")
        turned = sem("turned")
        hi_done = sem("hi_done")
        lo_done = sem("lo_done")
        stage_out = [sem(f"stage_out{i}") for i in range(STAGE_RING)]
        xT_stored = sem("xT_stored")
        gate_done = sem("gate_done")
        up_done = sem("up_done")
        silu_done = sem("silu_done")
        h_done = sem("h_done")
        hhi_done = sem("hhi_done")
        hlo_done = sem("hlo_done")
        down_done = sem("down_done")
        yscaled = sem("yscaled")
        g_done = sem("g_done")
        g_out = [sem(f"g_out{i}") for i in range(TPG)]

        def walk(tg):
            seen = []
            for c, events in enumerate(slots(tg)):
                for n, e in enumerate(events):
                    yield c, n, e, list(seen)
                    seen.append(e)

        def prologue_walk():
            for n, e in enumerate(prologue):
                yield 0, n, e, prologue[:n]

        def index(tg, seen, kinds="gudqox"):
            if tg is None:
                return count(seen, kinds)
            return before(tg, kinds) + count(seen, kinds)

        def ring(tg, seen, kinds, n):
            return count(seen, kinds) % n

        def uses(events, kinds, n, slot):
            return len(range(slot, count(events, kinds), n))

        def ring_uses(tg, seen, kinds, n, slot):
            within = uses(seen, kinds, n, slot)
            if tg is None:
                return within
            pro = uses(prologue, kinds, n, slot)
            if isinstance(tg, int) and tg == 0:
                return pro + within
            return (pro + uses(lists["first"], kinds, n, slot) + within
                    + (tg - 1) * uses(lists["middle"], kinds, n, slot))

        def previous(tg, seen, kinds, n):
            slot = ring(tg, seen, kinds, n)
            mine = [i for i, e in enumerate(seen) if e[0] in kinds]
            if len(mine) >= n:
                return (0 if tg is None else before(tg, "gudqox")) + mine[-n] + 1
            if tg is None:
                return None
            if isinstance(tg, int) and tg == 0:
                back, base = prologue, 0
            elif isinstance(tg, int) and tg == 1:
                back, base = lists["first"], before(0, "gudqox")
            else:
                return before(tg, "gudqox")
            mine = [i for i, e in enumerate(back) if e[0] in kinds]
            at = [i for k, i in enumerate(mine) if k % n == slot]
            return base + at[-1] + 1 if at else None

        def all_walks(engine, body, weights_are_in=lambda: None):
            body(None)
            body(0)
            weights_are_in()
            with engine.Fori(1, TG - 1) as tg:
                body(tg)
            body(TG - 1)

        block = ctx.enter_context(nc.Block())

        @block.gpsimd
        def _(pool):
            pool.memset(minus_half[:, :], -0.5).then_inc(ident_zero, 1)
            pool.memset(eps_col[:, :], EPS).then_inc(ident_zero, 1)
            pool.memset(ident[:, :], 0.0).then_inc(ident_zero, 1)
            pool.memset(ones[:, :], 1.0).then_inc(ones_ready, 1)
            pool.wait_ge(ident_zero, 3)
            pool.affine_select(out=ident[:, :], in_=ident[:, :], compare_op=ALU.not_equal, fill=1.0,
                               base=0, pattern=[[-1, P]], channel_multiplier=1).then_inc(ident_ready, 1)

            def rstd_of(n, slot):
                pool.wait_ge(moments_done, n + 1)
                pool.tensor_tensor(veps[:, slot, :], moments[:, slot, 1:2], eps_col[:, :], ALU.add).then_inc(veps_done, 1)
                pool.wait_ge(veps_done, n + 1)
                pool.tensor_tensor(rstd[:, slot, :], veps[:, slot, :], minus_half[:, :], ALU.pow).then_inc(rstd_done, 1)

            def low_of_h(n, s):
                pool.wait_ge(hhi_done, n + 1)
                pool.tensor_tensor(hT[:, s, 1, :], hf[:, s, :], hT[:, s, 0, :], ALU.subtract).then_inc(hlo_done, 1)

            def body(tg):
                events = prologue_walk() if tg is None else walk(tg)
                todo = {}
                for c, n, e, seen in events:
                    todo.setdefault(c, []).append((e, seen))
                for c in range(1 if tg is None else NC):
                    for e, seen in todo.get(c, []):
                        if e[0] == "x":
                            rstd_of(index(tg, seen, "x"), ring(tg, seen, "x", X_RING))
                    if tg is not None:
                        low_of_h(tg * NC + c, c % H_RING)

            all_walks(pool, body)

        @block.sync
        def _(sp):
            def load_scales():
                sp.dma_start(sd_row[:, :], sd.rearrange("(a n) -> a n", a=1).to_broadcast([P, DIM])).then_inc(scales_in, 16)
                with nc.allow_non_contiguous_dma(reason="two columns of scales, once"):
                    sp.dma_start(s_col[:, 0, :], sg.rearrange("(c p) -> p c", p=P)).then_inc(scales_in, 16)
                    sp.dma_start(s_col[:, 1, :], su.rearrange("(c p) -> p c", p=P)).then_inc(scales_in, 16)

            def load(tg, e, seen):
                kind, n = e
                prev = previous(tg, seen, "x" if kind == "x" else RAW, X_RING if kind == "x" else RAW_RING)
                if prev is not None:
                    sp.wait_ge(turned, prev)
                if kind == "x":
                    slot = ring(tg, seen, "x", X_RING)
                    tile = n if tg is None else (tg + 1) * TPG + n
                    sp.dma_start(xin[:, slot, :], x[tile]).then_inc(x_in[slot], 16)
                    return
                slot = ring(tg, seen, RAW, RAW_RING)
                done = 0 if tg is None or (isinstance(tg, int) and tg == 0) else before(tg, kind) if kind in "qo" else 0
                src = {"g": lambda: wg[n], "u": lambda: wu[n], "d": lambda: wd[n],
                       "q": lambda: wqkv[done + n], "o": lambda: wo[done + n]}[kind]()
                dst = raw[:, slot, :]
                if kind in "gud":
                    dst = dst.bitcast(I32)
                if kind in "do":
                    dst = dst.rearrange("p (r j) -> p r j", r=KC)
                sp.dma_start(dst, src).then_inc(raw_in[slot], 16)

            def store(tg, e, seen):
                kind, n = e
                if kind in STAGED:
                    slot = ring(tg, seen, STAGED, STAGE_RING)
                    done = 0 if isinstance(tg, int) and tg == 0 else before(tg, kind)
                    out = (wqkvT_out if kind == "q" else woT_out)[done + n]
                    sp.wait_ge(lo_done, index(tg, seen) + 1)
                    sp.dma_start(out, stage[:, slot].bitcast(F32)).then_inc(stage_out[slot], 16)
                if kind == "x" and n == TPG - 1:
                    group = 0 if tg is None else tg + 1
                    sp.wait_ge(lo_done, index(tg, seen) + 1)
                    sp.dma_start(xT_out[group], xT[:, group % 2].bitcast(F32)).then_inc(xT_stored, 16)

            def store_gate(tg, t):
                sp.wait_ge(g_done, tg * TPG + t + 1)
                sp.dma_start(gate_out[tg * TPG + t], gbuf[:, t, :]).then_inc(g_out[t], 16)

            def body(tg):
                events = [(c, e, seen) for c, _, e, seen in (prologue_walk() if tg is None else walk(tg))]
                if tg is None:
                    for k in range(AHEAD):
                        load(tg, *events[k][1:])
                elif not (isinstance(tg, int) and tg == 0):
                    for k in range(AHEAD):
                        load(tg, *events[k][1:])
                at = 0
                for c in range(1 if tg is None else NC):
                    while at < len(events) and events[at][0] == c:
                        if tg is None and at == len(events) - 1:
                            load_scales()
                            for _, e, seen in [(c, e, seen) for c, _, e, seen in walk(0)][:AHEAD]:
                                load(0, e, seen)
                        store(tg, *events[at][1:])
                        if at + AHEAD < len(events):
                            load(tg, *events[at + AHEAD][1:])
                        at += 1
                    if c == 0 and tg is not None and not (isinstance(tg, int) and tg == 0):
                        for t in range(TPG):
                            store_gate(tg - 1, t)

            all_walks(sp, body)
            for t in range(TPG):
                store_gate(TG - 1, t)
            staged = lists["first"] + lists["middle"] * 2 + lists["last"]
            for slot in range(STAGE_RING):
                n = sum(uses(ev, STAGED, STAGE_RING, slot) * k
                        for ev, k in ((lists["first"], 1), (lists["middle"], TG - 2), (lists["last"], 1)))
                sp.wait_ge(stage_out[slot], 16 * n)
            sp.wait_ge(xT_stored, 16 * TG)
            for t in range(TPG):
                sp.wait_ge(g_out[t], 16 * (TG + 1))

        def destination(tg, e, seen, part):
            kind, n = e
            if kind == "x":
                parity = 0 if tg is None else (tg + 1) % 2
                return xT[:, parity, n, part]
            if kind in "gu":
                return (wgT if kind == "g" else wuT)[:, part, :, n * P:(n + 1) * P]
            if kind == "d":
                return wdT[:, part, n, :].rearrange("p (c n) -> p c n", c=KC)
            return stage[:, ring(tg, seen, STAGED, STAGE_RING), part]

        def bank(tg, i):
            return (y[:, 0, :] if tg is None and i % 2 else prep[:, :]).rearrange("p (c n) -> p c n", c=KC)

        @block.scalar
        def _(act):
            def high(tg, e, seen):
                i = index(tg, seen)
                kind, n = e
                if kind in STAGED:
                    slot = ring(tg, seen, STAGED, STAGE_RING)
                    used = ring_uses(tg, seen, STAGED, STAGE_RING, slot)
                    if not isinstance(used, int) or used > 0:
                        act.wait_ge(stage_out[slot], 16 * used)
                if kind == "x" and n == 0 and tg is not None:
                    if isinstance(tg, int) and tg == 0:
                        pass
                    else:
                        act.wait_ge(gate_done, tg * NC)
                        act.wait_ge(up_done, tg * NC)
                        act.wait_ge(xT_stored, 16 * tg)
                act.wait_ge(turned, i + 1)
                act.copy(destination(tg, e, seen, 0), bank(tg, i)).then_inc(hi_done, 1)

            def silu(tg, c):
                n = tg * NC + c
                if isinstance(tg, int) and n == 0:
                    act.wait_ge(scales_in, 48)
                act.wait_ge(gate_done, n + 1)
                if c >= H_RING:
                    act.wait_ge(hlo_done, n - H_RING + 1)
                elif not (isinstance(tg, int) and tg == 0):
                    act.wait_ge(hlo_done, tg * NC)
                act.activation(hf[:, c % H_RING, :], gu[:, (2 * c) % GU_RING, :], ACT.Silu,
                               scale=s_col[:, 0, c:c + 1]).then_inc(silu_done, 1)

            def high_of_h(tg, c):
                n = tg * NC + c
                act.wait_ge(h_done, n + 1)
                if c >= H_RING:
                    act.wait_ge(down_done, n - H_RING + 1)
                elif not (isinstance(tg, int) and tg == 0):
                    act.wait_ge(down_done, tg * NC - (1 - c) if c else tg * NC)
                act.copy(hT[:, c % H_RING, 0, :], hf[:, c % H_RING, :]).then_inc(hhi_done, 1)

            def gates(tg):
                for t in range(TPG):
                    act.wait_ge(yscaled, tg * TPG + t + 1)
                    act.activation(gbuf[:, t, :], gbuf[:, t, :], ACT.Silu).then_inc(g_done, 1)

            def body(tg):
                todo = {}
                for c, n, e, seen in (prologue_walk() if tg is None else walk(tg)):
                    todo.setdefault(c, []).append((e, seen))
                if tg is None:
                    for e, seen in todo[0]:
                        high(tg, e, seen)
                    return
                for c in range(NC):
                    events = todo.get(c, [])
                    for k, step in enumerate((lambda: silu(tg, c), lambda: high_of_h(tg, c), lambda: None, lambda: None)):
                        if k < len(events):
                            high(tg, *events[k])
                        step()
                    if c == 0 and not (isinstance(tg, int) and tg == 0):
                        gates(tg - 1)

            all_walks(act, body)
            gates(TG - 1)

        @block.vector
        def _(dve):
            def ready(tg, e, seen):
                kind, n = e
                if kind in "gud":
                    slot = ring(tg, seen, RAW, RAW_RING)
                    used = ring_uses(tg, seen, RAW, RAW_RING, slot)
                    dve.wait_ge(raw_in[slot], 16 * (used + 1))
                    dve.tensor_scalar(raw[:, slot, :], raw[:, slot, :].bitcast(I32), -ZERO_POINT, None,
                                      ALU.add).then_inc(pre_done, 1)
                if kind == "x":
                    slot = ring(tg, seen, "x", X_RING)
                    k = index(tg, seen, "x")
                    dve.wait_ge(x_in[slot], 16 * (ring_uses(tg, seen, "x", X_RING, slot) + 1))
                    dve.bn_stats(stats[:, slot, :], xin[:, slot, :]).then_inc(stats_done, 1)
                    dve.wait_ge(stats_done, k + 1)
                    dve.tensor_copy(touched[:, :], stats[:, slot, 0:1])
                    dve.bn_aggr(moments[:, slot, :], stats[:, slot, :]).then_inc(moments_done, 1)
                    dve.wait_ge(rstd_done, k + 1)
                    dve.tensor_scalar(xin[:, slot, :], xin[:, slot, :], moments[:, slot, 0:1], rstd[:, slot, :],
                                      ALU.subtract, ALU.mult).then_inc(pre_done, 1)

            def low(tg, e, seen):
                i = index(tg, seen)
                dve.wait_ge(hi_done, i + 1)
                dve.tensor_tensor(destination(tg, e, seen, 1), bank(tg, i), destination(tg, e, seen, 0),
                                  ALU.subtract).then_inc(lo_done, 1)
                if e[0] in "gud":
                    dve.wait_ge(lo_done, i + 1)
                    n = count(prologue, "gud") + count(seen, "gud") if tg == 0 else count(seen, "gud")
                    part = destination(tg, e, seen, 1).bitcast(I32)
                    bits = low_bits.rearrange("p (c n) -> p c n", c=KC)
                    if n == 0:
                        dve.tensor_copy(bits, part).then_inc(bits_done, 1)
                    else:
                        dve.wait_ge(bits_done, n)
                        dve.tensor_tensor(bits, bits, part, ALU.bitwise_or).then_inc(bits_done, 1)

            def judge_weights():
                dve.wait_ge(bits_done, 3 * NC)
                dve.tensor_scalar(gbuf[:, 0, :], low_bits, 0.0, None, ALU.not_equal).then_inc(bits_done, 1)
                dve.wait_ge(bits_done, 3 * NC + 1)
                dve.tensor_reduce(any_low[:, :], gbuf[:, 0, :], AX_X, ALU.max).then_inc(any_low_done, 1)
                dve.wait_ge(counted, 1)
                dve.tensor_copy(wide[:, :], prep[:, 0:1]).then_inc(wide_done, 1)

            def gated(tg, c):
                n = tg * NC + c
                if isinstance(tg, int) and n == 0:
                    dve.wait_ge(scales_in, 48)
                dve.wait_ge(up_done, n + 1)
                dve.wait_ge(silu_done, n + 1)
                dve.scalar_tensor_tensor(hf[:, c % H_RING, :], gu[:, (2 * c + 1) % GU_RING, :], s_col[:, 1, c:c + 1],
                                         hf[:, c % H_RING, :], ALU.mult, ALU.mult).then_inc(h_done, 1)

            def scale_y(tg):
                dve.wait_ge(down_done, (tg + 1) * NC)
                for t in range(TPG):
                    dve.wait_ge(g_out[t], 16 * (tg + 1))
                    dve.tensor_tensor(gbuf[:, t, :], y[:, t, :], sd_row[:, :], ALU.mult).then_inc(yscaled, 1)

            def body(tg):
                todo = {}
                events = [(c, e, seen) for c, _, e, seen in (prologue_walk() if tg is None else walk(tg))]
                for c, e, seen in events:
                    todo.setdefault(c, []).append((e, seen))
                following = [(e, seen) for _, e, seen in events][1:]
                if tg is None:
                    ready(tg, *todo[0][0])
                    for e, seen in todo[0]:
                        if following:
                            ready(tg, *following.pop(0))
                        low(tg, e, seen)
                    return
                ready(tg, *events[0][1:])
                for c in range(NC):
                    slot_events = todo.get(c, [])
                    for k in range(4):
                        if k < len(slot_events):
                            if following:
                                ready(tg, *following.pop(0))
                            low(tg, *slot_events[k])
                        if k == 1:
                            gated(tg, c)
                    if c == 0 and not (isinstance(tg, int) and tg == 0):
                        scale_y(tg - 1)

            for t in range(TPG):
                dve.sem_inc(g_out[t], 16)
            all_walks(dve, body, judge_weights)
            scale_y(TG - 1)

        @block.tensor
        def _(pe):
            pe.wait_ge(ident_ready, 1)

            def turn(tg, e, seen):
                kind, n = e
                if kind in PRE:
                    pe.wait_ge(pre_done, index(tg, seen, PRE) + 1)
                else:
                    slot = ring(tg, seen, RAW, RAW_RING)
                    pe.wait_ge(raw_in[slot], 16 * (ring_uses(tg, seen, RAW, RAW_RING, slot) + 1))
                i = index(tg, seen)
                if tg is not None:
                    pe.wait_ge(lo_done, i)
                elif i >= 2:
                    pe.wait_ge(lo_done, i - 1)
                src = xin[:, ring(tg, seen, "x", X_RING), :] if kind == "x" else raw[:, ring(tg, seen, RAW, RAW_RING), :]
                for k in range(KC):
                    last = pe.transpose(bank(tg, i)[:, k, :], src[:, k * P:(k + 1) * P], ident[:, :])
                last.then_inc(turned, 1)

            def hidden(tg, c, side, low_weights):
                w = (wgT, wuT)[side]
                use = 2 * c + side
                if use >= GU_RING:
                    n = tg * NC + (use - GU_RING) // 2
                    pe.wait_ge(silu_done if (use - GU_RING) % 2 == 0 else h_done, n + 1)
                elif not (isinstance(tg, int) and tg == 0):
                    pe.wait_ge(silu_done, tg * NC)
                    pe.wait_ge(h_done, tg * NC)
                out = gu[:, use % GU_RING, :].rearrange("p (t n) -> p t n", t=TPG)
                parity = tg % 2
                passes = ((0, 0), (0, 1), (1, 0)) if low_weights else ((0, 0), (0, 1))
                for k in range(KC):
                    for n, (wp, xp) in enumerate(passes):
                        last = pe.matmul(out, w[:, wp, k, c * P:(c + 1) * P], xT[:, parity, :, xp, k, :],
                                         start=k == n == 0, stop=k == KC - 1 and n == len(passes) - 1)
                last.then_inc(up_done if side else gate_done, 1)

            def down(tg, c, half, low_weights):
                if half == 0:
                    pe.wait_ge(hlo_done, tg * NC + c + 1)
                if half == c == 0 and not (isinstance(tg, int) and tg == 0):
                    pe.wait_ge(yscaled, tg * TPG)
                for t in range(half * TPG // 2, (half + 1) * TPG // 2):
                    passes = ((0, 0), (0, 1), (1, 0)) if low_weights else ((0, 0), (1, 0))
                    for n, (hp, wp) in enumerate(passes):
                        last = pe.matmul(y[:, t, :], hT[:, c % H_RING, hp, t * P:(t + 1) * P], wdT[:, wp, c, :],
                                         start=c == n == 0, stop=c == NC - 1 and n == len(passes) - 1)
                if half == 1:
                    last.then_inc(down_done, 1)

            def body(tg, low_weights=True):
                todo = {}
                for c, n, e, seen in (prologue_walk() if tg is None else walk(tg)):
                    todo.setdefault(c, []).append((e, seen))
                if tg is None:
                    for e, seen in todo[0]:
                        turn(tg, e, seen)
                    pe.wait_ge(lo_done, len(prologue))
                    return
                for c in range(NC):
                    events = todo.get(c, [])
                    if c == 0:
                        pe.wait_ge(lo_done, before(tg, "gudqox"))
                    elif isinstance(tg, int) and tg == 0:
                        pe.wait_ge(lo_done, before(0, "gudqox") + sum(len(s) for s in FIRST[:c]))
                    steps = [lambda: hidden(tg, c, 0, low_weights), lambda: hidden(tg, c, 1, low_weights)]
                    if c > 0:
                        steps += [lambda: down(tg, c - 1, 0, low_weights), lambda: down(tg, c - 1, 1, low_weights)]
                    elif not (isinstance(tg, int) and tg == 0):
                        steps += [lambda: down(tg - 1, NC - 1, 0, low_weights), lambda: down(tg - 1, NC - 1, 1, low_weights)]
                    for k in range(max(len(steps), len(events))):
                        if k < len(events):
                            turn(tg, *events[k])
                        if k < len(steps):
                            steps[k]()

            def after_first(low_weights):
                with pe.Fori(1, TG - 1) as tg:
                    body(tg, low_weights)
                body(TG - 1, low_weights)
                for half in range(2):
                    down(TG - 1, NC - 1, half, low_weights)

            body(None)
            body(0)
            pe.wait_ge(ones_ready, 1)
            pe.wait_ge(any_low_done, 1)
            pe.wait_ge(lo_done, len(prologue) + len(lists["first"]))
            pe.matmul(prep[:, 0:1], ones[:, :], any_low[:, :], start=True, stop=True).then_inc(counted, 1)
            pe.wait_ge(wide_done, 1)
            has_low = pe.alloc_register("has_low")
            pe.reg_load(has_low, wide[0:1, 0:1])
            with pe.If_ne(has_low, 0):
                after_first(True)
            with pe.Else():
                after_first(False)
            pe.end_ifs()


QT = 4
UNITS = 2 * REP
HALF = NST // 2
HEAD_RING = 4
LAG = 2
PT_RING = 3
MASKED = -3.0e38


def blocks_of(u):
    return QT * (u // REP + 1)


def blocks_before(u):
    return sum(blocks_of(v) for v in range(u))


BLOCKS = blocks_before(UNITS)

STEPS = ("qkv", "stats", "norm", "affine", "rope", "turn")
OPENING_LATE = ((0, 1, 3, 4, 6, 7), (0, 1, 3, 4, 6, 7), (0, 1, 3, 4, 6, 7), (0, 1, 3, 4, 6, 7))
NEXT_LATE = ((0, 1, 2, 3, 5, 7), (0, 1, 2, 3, 5, 7), (0, 1, 2, 3, 5, 7), (0, 1, 2, 3, 5, 7))
SECOND_LATE = ((0, 1, 2, 3, 5, 6), (0, 1, 2, 3, 5, 7), (0, 1, 2, 3, 5, 7), (0, 1, 2, 3, 5, 6))
NEXT_AT = (17, 22, 27, 30)
SECOND_AT = (1, 2, 3, 6)
OUT_AT = (19, 21, 22, 24)
S_AT = ((0, 0, 1, 1), (0, 1, 2, 3))
NEXT_S_AT = (1, 2, 8, 8)
WEIGHTS_LATE = 1
FIRST_T_PLACE = (0, 0, 0, 0, 3, 0, 0, 1)
ORDER = {kind: m for m, kind in enumerate(('turn', 'norm', 'rope', 'stats', 'affine', 'qkv', 'out'))}


def token_tiles(tiles, at, late):
    return [(start + lag, (kind, n)) for n, start, lags in zip(tiles, at, late)
            for kind, lag in zip(STEPS, lags)]


def opening():
    placed = sorted(token_tiles(range(HALF), (0, 2, 4, 6), OPENING_LATE), key=lambda p: (p[0], ORDER[p[1][0]]))
    return with_weights([step for _, step in placed] + [("spare_k",)] + [("S", 0, t) for t in range(QT)]
                        + [("spare_v",)])


def with_weights(steps):
    due, placed = [], []
    at = 0
    for step in steps:
        if step[0] == "T":
            ready = [e for e in due if at - e[2] >= WEIGHTS_LATE or (e[0] == step[1] and step[2] == 0)]
            placed += [("P", *e[:2]) for e in ready]
            due = [e for e in due if e not in ready]
            at += 1
        if step == ("out", QT + 1):
            placed += [("P", *e[:2]) for e in due]
            due = []
        placed.append(step)
        if step[0] == "S":
            due.append((*step[1:], at))
    return placed + [("P", *e[:2]) for e in due]


def maxima_first(steps):
    steps, at = list(steps), 0
    while at + 1 < len(steps):
        if steps[at][0][0] == "T" and steps[at + 1][0][0] == "S":
            steps[at], steps[at + 1] = steps[at + 1], steps[at]
        at += 1
    return steps


def schedule(another):
    beside = token_tiles(range(HALF, NST), SECOND_AT, SECOND_LATE)
    if another:
        beside += token_tiles(range(HALF), NEXT_AT, NEXT_LATE)
    beside += [(at, ("out", t)) for t, at in enumerate(OUT_AT)]
    blocks = [(u, j) for u in range(UNITS) for j in range(blocks_of(u))]
    steps = []
    for k, (u, j) in enumerate(blocks):
        scores, values = [], []
        if another and (u, j) == (UNITS - 1, 0):
            scores.append(("spare_k",))
        if u + 1 < UNITS or another:
            where = S_AT[(u + 1) // REP] if u + 1 < UNITS else NEXT_S_AT
            scores += [("S", (u + 1) % UNITS, t) for t in range(QT) if where[t] == j]
        if k >= LAG:
            values.append(("PV", *blocks[k - LAG]))
            if another and blocks[k - LAG] == (UNITS - 1, HALF - 1):
                values.append(("spare_v",))
        parts = [scores, sorted((step for at, step in beside if at == k), key=lambda e: ORDER[e[0]]), values]
        parts.insert(FIRST_T_PLACE[u] if j == 0 else 0, [("T", u, j)])
        steps += [step for part in parts for step in part]
    steps += [("PV", *e) for e in blocks[-LAG:]]
    if another:
        steps += [("S", 0, t) for t in range(QT) if NEXT_S_AT[t] >= HALF + QT]
    steps += [("out", QT + t) for t in range(QT)]
    return with_weights(steps)


def attention_block(nc, dram, scratch, out):
    x, cos, ssin, norms = (dram[k] for k in ("x", "cos", "ssin", "norms"))
    xT_in, wqkvT_in, woT_in, gate_in = scratch
    HEADS = REP + 1
    ctx = ExitStack()
    with ctx:
        def sb(name, shape, dt=F32):
            return ctx.enter_context(nc.sbuf_tensor(name, shape, dt))

        def sem(name):
            return ctx.enter_context(nc.semaphore(name))

        wT = sb("wT", [P, 2, KC, KV_COLS], F32R)
        woT = sb("woT", [P, 2, REP, DIM], F32R)
        xt = sb("xt", [P, 2, 2, KC, P], F32R)
        qk = sb("qk", [P, 2, HEADS, S], F32R)
        v = sb("v", [P, 2, NST, D], F32R)
        k_spare = sb("k_spare", [P, 2, HALF * P], F32R)
        v_spare = sb("v_spare", [P, 2, HALF, D], F32R)
        pbuf = sb("pbuf", [P, 2, sum(QT + t + 1 for t in range(QT)) * P])
        pT = sb("pT", [P, PT_RING, 2, QT * P], F32R)
        aT = sb("aT", [P, 2, REP, QT * P], F32R)
        yacc = sb("yacc", [P, NST, DIM])
        cos_sb = sb("cos_sb", [P, NST, D // 2])
        ssin_sb = sb("ssin_sb", [P, NST, D])
        rows = sb("rows", [P, 2, HEADS, D])
        heads = sb("heads", [P, HEAD_RING, QK_COLS])
        rotated = sb("rotated", [P, QK_COLS])
        xg = sb("xg", [P, 2, 2, DIM])
        ident = sb("ident2", [P, P])
        identb = sb("identb", [P, P], BF16)
        maskb = sb("maskb", [P, P], BF16)
        zeros = sb("zeros", [P, P])
        stats = sb("stats2", [P, 2, HEADS, 6])
        moments = sb("moments2", [P, 2, HEADS, 2])
        veps = sb("veps2", [P, 2, HEADS])
        rstd = sb("rstd2", [P, 2, HEADS])
        nbias = sb("nbias", [P, 2, HEADS])
        minus_half = sb("minus_half2", [P, 1])
        minus_one = sb("minus_one", [P, 1])
        eps_col = sb("eps_col2", [P, 1])
        touched = sb("touched2", [P, 1])
        nmax = sb("nmax", [P, 2, QT])
        lsum = sb("lsum", [P, 2, QT])
        linv = sb("linv", [P, 2, QT])
        mask = pbuf[:, 1, 0:P]

        s_ps = ctx.enter_context(nc.psum_tensor("s_ps", [P, 2, S], F32))
        t_ps = ctx.enter_context(nc.psum_tensor("t_ps", [P, 2, QT * P], F32))
        o_ps = ctx.enter_context(nc.psum_tensor("o_ps", [P, 2, QT * P], F32))

        consts_made = sem("consts_made")
        consts_ready = sem("consts_ready")
        tables_in = sem("tables_in")
        rows_ready = sem("rows_ready")
        w_in = sem("w_in")
        wo_in = sem("wo_in")
        xt_in = [sem(f"xt_in{i}") for i in range(2)]
        qkv_done = sem("qkv_done")
        stats_done = sem("stats_done2")
        moments_done = sem("moments_done2")
        veps_done = sem("veps_done2")
        rstd_done = sem("rstd_done2")
        nbias_done = sem("nbias_done")
        norm_done = sem("norm_done")
        vhi_done = sem("vhi_done")
        vlo_done = sem("vlo_done")
        raw_done = sem("raw_done")
        scaled = sem("scaled")
        shifted = sem("shifted")
        affine_done = sem("affine_done")
        cosed = sem("cosed")
        rope_done = sem("rope_done")
        turned = sem("turned2")
        qkhi_done = sem("qkhi_done")
        qklo_done = sem("qklo_done")
        khi_moved = sem("khi_moved")
        klo_moved = sem("klo_moved")
        v_free = sem("v_free")
        vhi_moved = sem("vhi_moved")
        vlo_moved = sem("vlo_moved")
        s_done = sem("s_done")
        max_done = sem("max_done")
        exp_done = sem("exp_done")
        linv_done = sem("linv_done")
        p_done = sem("p_done")
        pt_turned = sem("pt_turned")
        pthi_done = sem("pthi_done")
        ptlo_done = sem("ptlo_done")
        pv_done = sem("pv_done")
        ahi_done = sem("ahi_done")
        alo_done = sem("alo_done")
        out_done = sem("out_done")
        added = sem("added")
        yzero = sem("yzero")
        xg_in = [sem(f"xg_in{i}") for i in range(2)]
        gated = sem("gated")
        fin_done = sem("fin_done")
        stored = [sem(f"stored{i}") for i in range(2)]

        def every_head(engine, body):
            body(-1, True, False)
            for b in range(B):
                with engine.Fori(b * HKV, (b + 1) * HKV - 1) as it:
                    body(it, True, False)
                body((b + 1) * HKV - 1, b + 1 < B, True)

        def steps_of(it, another):
            steps = opening() if isinstance(it, int) and it < 0 else schedule(another)
            held = [("S", 0, QT - 2), ("S", 0, QT - 1)]
            if isinstance(it, int) and it < 0:
                held = [None, None]
            at = 0
            for step in steps:
                slot = last = None
                if step[0] in ("S", "qkv", "turn"):
                    slot, last = at % 2, (held[at % 2], at < 2)
                    held[at % 2] = step
                    at += 1
                yield step, slot, last

        def tile_count(it, n):
            return HALF + it * NST + (n + HALF) % NST

        def s_count(it, u, t):
            return it * (UNITS * QT) + (u * QT + t if u else UNITS * QT + t)

        def cols(t, u):
            return (QT * (u // REP) + t + 1) * P

        def weights(u, t, c0, c1):
            at = sum(QT + s + 1 for s in range(t)) * P
            return pbuf[:, u % 2, at + c0:at + c1]

        def first_col(u, j):
            r = j - QT * (u // REP)
            return min(max(r, 0), 2) * P

        def out_bank(i):
            return 1 if i < QT else i % 2

        def k_place(n, part):
            if n < HALF:
                return k_spare[:, part, n * P:(n + 1) * P]
            return qk[:, part, REP, n * P:(n + 1) * P]

        def v_place(n, part):
            return v_spare[:, part, n, :] if n < HALF else v[:, part, n, :]

        def results_before(it):
            return (it // HKV) * NST

        block = ctx.enter_context(nc.Block())

        @block.sync
        def _(sp):
            def load_w(kv):
                for s, tile in enumerate([kv * REP + h for h in range(REP)] + [H + kv, H + HKV + kv]):
                    sp.dma_start(wT[:, :, :, s * D:(s + 1) * D].bitcast(F32), wqkvT_in[tile]).then_inc(w_in, 16)

            def load_x(it, b, n):
                k = tile_count(it, n)
                if not (isinstance(k, int) and k < 2):
                    sp.wait_ge(qkv_done, k - 1)
                sp.dma_start(xt[:, n % 2].bitcast(F32), xT_in[b * (TG // B) + n // TPG, :, n % TPG]).then_inc(xt_in[n % 2], 16)

            load_w(0)
            load_x(-1, 0, 0)
            load_x(-1, 0, 1)
            for part in range(2):
                for dst, src in ((rows[:, part, 0:REP, :], norms[part]), (rows[:, part, REP:HEADS, :], norms[2 + part])):
                    sp.dma_start(dst, src.rearrange("(o a d) -> o a d", o=1, a=1).to_broadcast([P, dst.shape[1], D])).then_inc(tables_in, 16)
            sp.dma_start(cos_sb[:, :, :], cos).then_inc(tables_in, 16)
            sp.dma_start(ssin_sb[:, :, :], ssin).then_inc(tables_in, 16)
            load_x(-1, 0, 2)
            load_x(-1, 0, 3)

            def head(it, b, another, final):
                kv = it - b * HKV
                load_x(it, b, HALF)
                load_x(it, b, HALF + 1)
                sp.wait_ge(out_done, 1 + it * NST)
                for h in range(REP):
                    sp.dma_start(woT[:, :, h, :].bitcast(F32), woT_in[kv * REP + h]).then_inc(wo_in, 16)
                load_x(it, b, HALF + 2)
                load_x(it, b, HALF + 3)
                if final:
                    load_result(it, 0)
                    load_result(it, 1)
                if another:
                    sp.wait_ge(qkv_done, tile_count(it, NST - 1) + 1)
                    load_w(0 if final else kv + 1)
                    for n in range(HALF):
                        load_x(it, b + 1 if final else b, n)
                if final:
                    for i in range(NST):
                        k = results_before(it) + i
                        sp.wait_ge(fin_done, k + 1)
                        sp.dma_start(out[k], xg[:, i % 2, 0, :]).then_inc(stored[i % 2], 16)
                        if i + 2 < NST:
                            load_result(it, i + 2)

            def load_result(it, i):
                k = results_before(it) + i
                if k >= 2:
                    sp.wait_ge(stored[i % 2], 16 * (k // 2))
                sp.dma_start(xg[:, i % 2, 0, :], x[k]).then_inc(xg_in[i % 2], 16)
                sp.dma_start(xg[:, i % 2, 1, :], gate_in[k]).then_inc(xg_in[i % 2], 16)

            for b in range(B):
                with sp.Fori(b * HKV, (b + 1) * HKV - 1) as it:
                    head(it, b, True, False)
                head((b + 1) * HKV - 1, b, b + 1 < B, True)
            for i in range(2):
                sp.wait_ge(stored[i], 16 * (B * NST // 2))

        @block.gpsimd
        def _(pool):
            pool.memset(ident[:, :], 0.0).then_inc(consts_made, 1)
            pool.memset(mask, 0.0).then_inc(consts_made, 1)
            pool.memset(zeros[:, :], 0.0).then_inc(consts_made, 1)
            pool.memset(minus_half[:, :], -0.5).then_inc(consts_made, 1)
            pool.memset(minus_one[:, :], -1.0).then_inc(consts_made, 1)
            pool.memset(eps_col[:, :], EPS).then_inc(consts_made, 1)
            pool.wait_ge(consts_made, 6)
            pool.affine_select(out=ident[:, :], in_=ident[:, :], compare_op=ALU.not_equal, fill=1.0,
                               base=0, pattern=[[-1, P]], channel_multiplier=1).then_inc(consts_made, 1)
            pool.affine_select(out=mask, in_=mask, compare_op=ALU.is_ge, fill=MASKED,
                               base=0, pattern=[[-1, P]], channel_multiplier=1).then_inc(consts_made, 1)
            pool.wait_ge(consts_made, 8)
            pool.tensor_copy(identb[:, :], ident[:, :]).then_inc(consts_ready, 1)
            pool.tensor_copy(maskb[:, :], mask).then_inc(consts_ready, 1)
            pool.memset(yacc[:, :, :], 0.0).then_inc(yzero, 1)
            pool.wait_ge(rows_ready, 2)

            def body(it, another, final):
                for (kind, *a), _, _ in steps_of(it, another):
                    if kind == "stats":
                        n, = a
                        k = tile_count(it, n)
                        pool.wait_ge(moments_done, k + 1)
                        if not (isinstance(k, int) and k < 2):
                            pool.wait_ge(norm_done, k - 1)
                        pool.tensor_tensor(veps[:, n % 2, :], moments[:, n % 2, :, 1],
                                           eps_col[:, :].to_broadcast([P, HEADS]), ALU.add).then_inc(veps_done, 1)
                        pool.wait_ge(veps_done, k + 1)
                        pool.tensor_tensor(rstd[:, n % 2, :], veps[:, n % 2, :],
                                           minus_half[:, :].to_broadcast([P, HEADS]), ALU.pow).then_inc(rstd_done, 1)
                    if kind == "affine":
                        n, = a
                        k = tile_count(it, n)
                        y = heads[:, n % HEAD_RING, :].rearrange("p (h d) -> p h d", d=D)
                        pool.wait_ge(scaled, k + 1)
                        pool.tensor_tensor(y, y, rows[:, 1], ALU.add).then_inc(shifted, 1)
                        pool.wait_ge(shifted, k + 1)
                        if not (isinstance(k, int) and k < 1):
                            pool.wait_ge(rope_done, k)
                        y = heads[:, n % HEAD_RING, :].rearrange("p (h s d) -> p h s d", s=2, d=D // 2)
                        r = rotated[:, :].rearrange("p (h s d) -> p h s d", s=2, d=D // 2)
                        for s in range(2):
                            sine = ssin_sb[:, n:n + 1, s * (D // 2):(s + 1) * (D // 2)].to_broadcast([P, HEADS, D // 2])
                            last = pool.tensor_tensor(r[:, :, s, :], y[:, :, 1 - s, :], sine, ALU.mult)
                        last.then_inc(affine_done, 1)
                    if kind == "S":
                        u, t = a
                        k = s_count(it, u, t)
                        pool.wait_ge(exp_done, k + 1)
                        pool.tensor_tensor(linv[:, u % 2, t:t + 1], lsum[:, u % 2, t:t + 1], minus_one[:, :],
                                           ALU.pow).then_inc(linv_done, 1)

            every_head(pool, body)

        @block.scalar
        def _(act):
            def body(it, another, final):
                for (kind, *a), slot, _ in steps_of(it, another):
                    if kind == "qkv":
                        n, = a
                        k = tile_count(it, n)
                        act.wait_ge(qkv_done, k + 1)
                        act.copy(v_place(n, 0), s_ps[:, slot, QK_COLS:KV_COLS]).then_inc(vhi_done, 1)
                        if not (isinstance(k, int) and k < HEAD_RING):
                            act.wait_ge(turned, k - HEAD_RING + 1)
                        act.copy(heads[:, n % HEAD_RING, :], s_ps[:, slot, 0:QK_COLS]).then_inc(raw_done, 1)
                    if kind == "norm":
                        n, = a
                        k = tile_count(it, n)
                        act.wait_ge(nbias_done, k + 1)
                        for h in range(HEADS):
                            y = heads[:, n % HEAD_RING, h * D:(h + 1) * D]
                            last = act.activation(y, y, ACT.Identity, bias=nbias[:, n % 2, h:h + 1], scale=rstd[:, n % 2, h:h + 1])
                        last.then_inc(norm_done, 1)
                    if kind == "turn":
                        n, = a
                        act.wait_ge(turned, tile_count(it, n) + 1)
                        src = s_ps[:, slot, 0:QK_COLS].rearrange("p (h t) -> p h t", t=P)
                        act.copy(qk[:, 0, 0:REP, n * P:(n + 1) * P], src[:, 0:REP, :])
                        act.copy(k_place(n, 0), src[:, REP, :]).then_inc(qkhi_done, 1)
                    if kind == "spare_k":
                        act.wait_ge(qkhi_done, tile_count(it, HALF - 1) + 1)
                        if not (isinstance(it, int) and it < 0):
                            act.wait_ge(s_done, s_count(it, UNITS - 1, QT - 1) + 1)
                        act.copy(qk[:, 0, REP, 0:HALF * P], k_spare[:, 0, :]).then_inc(khi_moved, 1)
                    if kind == "spare_v":
                        act.wait_ge(vhi_done, tile_count(it, HALF - 1) + 1)
                        if not (isinstance(it, int) and it < 0):
                            act.wait_ge(v_free, it + 1)
                        act.copy(v[:, 0, 0:HALF, :], v_spare[:, 0]).then_inc(vhi_moved, 1)
                    if kind == "S":
                        u, t = a
                        act.wait_ge(max_done, s_count(it, u, t) + 1)
                        act.activation(weights(u, t, 0, cols(t, u)), s_ps[:, slot, 0:cols(t, u)], ACT.Exp,
                                       bias=nmax[:, u % 2, t:t + 1], scale=1.0,
                                       accum_out=lsum[:, u % 2, t:t + 1]).then_inc(exp_done, 1)
                    if kind == "T":
                        u, j = a
                        k, c = blocks_before(u) + j, first_col(u, j)
                        act.wait_ge(pt_turned, it * BLOCKS + k + 1)
                        act.copy(pT[:, k % PT_RING, 0, c:], t_ps[:, k % 2, c:]).then_inc(pthi_done, 1)
                    if kind == "PV" and a[1] == blocks_of(a[0]) - 1:
                        u = a[0]
                        act.wait_ge(pv_done, it * UNITS + u + 1)
                        act.copy(aT[:, 0, u % REP, :], o_ps[:, u % 2, :]).then_inc(ahi_done, 1)

            act.wait_ge(consts_ready, 2)
            every_head(act, body)

        @block.vector
        def _(dve):
            dve.sem_inc(added, 1)
            dve.wait_ge(tables_in, 96)
            for part in range(2):
                dve.tensor_scalar(rows[:, part, 0:REP, :], rows[:, part, 0:REP, :], D ** -0.5, None,
                                  ALU.mult).then_inc(rows_ready, 1)
            dve.wait_ge(yzero, 1)

            def body(it, another, final):
                for (kind, *a), slot, _ in maxima_first(steps_of(it, another)):
                    if kind == "qkv":
                        n, = a
                        k = tile_count(it, n)
                        dve.wait_ge(vhi_done, k + 1)
                        dve.wait_ge(raw_done, k + 1)
                        dve.tensor_tensor(v_place(n, 1), s_ps[:, slot, QK_COLS:KV_COLS], v_place(n, 0),
                                          ALU.subtract).then_inc(vlo_done, 1)
                    if kind == "stats":
                        n, = a
                        k = tile_count(it, n)
                        for h in range(HEADS):
                            last = dve.bn_stats(stats[:, n % 2, h, :], heads[:, n % HEAD_RING, h * D:(h + 1) * D])
                        last.then_inc(stats_done, 1)
                        dve.wait_ge(stats_done, k + 1)
                        dve.tensor_copy(touched[:, :], stats[:, n % 2, HEADS - 1, 0:1])
                        for h in range(HEADS):
                            last = dve.bn_aggr(moments[:, n % 2, h, :], stats[:, n % 2, h, :])
                        last.then_inc(moments_done, 1)
                    if kind == "norm":
                        n, = a
                        k = tile_count(it, n)
                        dve.wait_ge(rstd_done, k + 1)
                        if not (isinstance(k, int) and k < 2):
                            dve.wait_ge(norm_done, k - 1)
                        dve.scalar_tensor_tensor(nbias[:, n % 2, :], moments[:, n % 2, :, 0], -1.0, rstd[:, n % 2, :],
                                                 ALU.mult, ALU.mult).then_inc(nbias_done, 1)
                    if kind == "affine":
                        n, = a
                        y = heads[:, n % HEAD_RING, :].rearrange("p (h d) -> p h d", d=D)
                        dve.wait_ge(norm_done, tile_count(it, n) + 1)
                        dve.tensor_tensor(y, y, rows[:, 0], ALU.mult).then_inc(scaled, 1)
                    if kind == "rope":
                        n, = a
                        k = tile_count(it, n)
                        y = heads[:, n % HEAD_RING, :]
                        dve.wait_ge(affine_done, k + 1)
                        dve.tensor_tensor(y.rearrange("p (h d) -> p h d", d=D // 2), y.rearrange("p (h d) -> p h d", d=D // 2),
                                          cos_sb[:, n:n + 1, :].to_broadcast([P, 2 * HEADS, D // 2]), ALU.mult).then_inc(cosed, 1)
                        dve.wait_ge(cosed, k + 1)
                        dve.tensor_tensor(y, y, rotated[:, :], ALU.add).then_inc(rope_done, 1)
                    if kind == "turn":
                        n, = a
                        dve.wait_ge(qkhi_done, tile_count(it, n) + 1)
                        src = s_ps[:, slot, 0:QK_COLS].rearrange("p (h t) -> p h t", t=P)
                        here = qk[:, :, 0:REP, n * P:(n + 1) * P]
                        dve.tensor_tensor(here[:, 1], src[:, 0:REP, :], here[:, 0], ALU.subtract)
                        dve.tensor_tensor(k_place(n, 1), src[:, REP, :], k_place(n, 0), ALU.subtract).then_inc(qklo_done, 1)
                    if kind == "spare_k":
                        dve.wait_ge(qklo_done, tile_count(it, HALF - 1) + 1)
                        if not (isinstance(it, int) and it < 0):
                            dve.wait_ge(s_done, s_count(it, UNITS - 1, QT - 1) + 1)
                        dve.tensor_copy(qk[:, 1, REP, 0:HALF * P], k_spare[:, 1, :]).then_inc(klo_moved, 1)
                    if kind == "spare_v":
                        dve.wait_ge(vlo_done, tile_count(it, HALF - 1) + 1)
                        if not (isinstance(it, int) and it < 0):
                            dve.wait_ge(v_free, it + 1)
                        dve.tensor_copy(v[:, 1, 0:HALF, :], v_spare[:, 1]).then_inc(vlo_moved, 1)
                    if kind == "S":
                        u, t = a
                        dve.wait_ge(s_done, s_count(it, u, t) + 1)
                        dve.tensor_reduce(nmax[:, u % 2, t:t + 1], s_ps[:, slot, 0:cols(t, u)], AX_X, ALU.max,
                                          negate=True).then_inc(max_done, 1)
                    if kind == "P":
                        u, t = a
                        dve.wait_ge(linv_done, s_count(it, u, t) + 1)
                        w = weights(u, t, 0, cols(t, u))
                        dve.tensor_scalar(w, w, linv[:, u % 2, t:t + 1], None, ALU.mult).then_inc(p_done, 1)
                    if kind == "T":
                        u, j = a
                        k, c = blocks_before(u) + j, first_col(u, j)
                        dve.wait_ge(pthi_done, it * BLOCKS + k + 1)
                        dve.tensor_tensor(pT[:, k % PT_RING, 1, c:], t_ps[:, k % 2, c:], pT[:, k % PT_RING, 0, c:],
                                          ALU.subtract).then_inc(ptlo_done, 1)
                    if kind == "PV" and a[1] == blocks_of(a[0]) - 1:
                        u = a[0]
                        dve.wait_ge(ahi_done, it * UNITS + u + 1)
                        dve.tensor_tensor(aT[:, 1, u % REP, :], o_ps[:, u % 2, :], aT[:, 0, u % REP, :],
                                          ALU.subtract).then_inc(alo_done, 1)
                    if kind == "out":
                        i, = a
                        dve.wait_ge(out_done, 1 + it * NST + i + 1)
                        dve.tensor_tensor(yacc[:, i, :], yacc[:, i, :], o_ps[:, out_bank(i), :], ALU.add).then_inc(added, 1)
                        if final:
                            k = results_before(it) + i
                            dve.wait_ge(added, 1 + it * NST + i + 1)
                            dve.wait_ge(xg_in[i % 2], 32 * (k // 2 + 1))
                            dve.tensor_tensor(yacc[:, i, :], yacc[:, i, :], xg[:, i % 2, 1, :], ALU.mult).then_inc(gated, 1)
                            dve.wait_ge(gated, k + 1)
                            dve.tensor_tensor(xg[:, i % 2, 0, :], yacc[:, i, :], xg[:, i % 2, 0, :], ALU.add).then_inc(fin_done, 1)
                            if another:
                                dve.wait_ge(fin_done, k + 1)
                                dve.memset(yacc[:, i, :], 0.0)

            every_head(dve, body)

        @block.tensor
        def _(pe):
            pe.sem_inc(out_done, 1)
            pe.wait_ge(consts_ready, 2)

            def wait_for_slot(it, last):
                step, earlier = last
                if step is None:
                    return
                kind, *a = step
                it = it - 1 if earlier else it
                if kind == "S":
                    pe.wait_ge(exp_done, s_count(it, *a) + 1)
                if kind == "qkv":
                    pe.wait_ge(vlo_done, tile_count(it, *a) + 1)
                if kind == "turn":
                    pe.wait_ge(qklo_done, tile_count(it, *a) + 1)

            def body(it, another, final):
                for (kind, *a), slot, last_use in steps_of(it, another):
                    if slot is not None:
                        wait_for_slot(it, last_use)
                    if kind == "qkv":
                        n, = a
                        k = tile_count(it, n)
                        if n == 0:
                            pe.wait_ge(w_in, (it + 2) * (16 * (REP + 2)))
                        pe.wait_ge(xt_in[n % 2], (it * (NST // 2) + HALF // 2 + ((n + HALF) % NST) // 2 + 1) * 16)
                        for c in range(KC):
                            for xp, wp in ((0, 0), (0, 1), (1, 0)):
                                lhs = xt[:, n % 2, xp, c, :]
                                first, final_one = c == 0 and xp == wp == 0, c == KC - 1 and xp == 1
                                pe.matmul(s_ps[:, slot, 0:REP * D], lhs, wT[:, wp, c, 0:REP * D], start=first, stop=final_one)
                                last = pe.matmul(s_ps[:, slot, REP * D:KV_COLS], lhs, wT[:, wp, c, REP * D:],
                                                 start=first, stop=final_one)
                        last.then_inc(qkv_done, 1)
                    if kind == "turn":
                        n, = a
                        pe.wait_ge(rope_done, tile_count(it, n) + 1)
                        for h in range(HEADS):
                            last = pe.transpose(s_ps[:, slot, h * P:(h + 1) * P], heads[:, n % HEAD_RING, h * D:(h + 1) * D], ident[:, :])
                        last.then_inc(turned, 1)
                    if kind == "S":
                        u, t = a
                        h, i = u % REP, QT * (u // REP) + t
                        if u == 0 and t == 0:
                            pe.wait_ge(qklo_done, tile_count(it, HALF - 1) + 1)
                            pe.wait_ge(khi_moved, it + 2)
                            pe.wait_ge(klo_moved, it + 2)
                        if u == REP:
                            pe.wait_ge(qklo_done, tile_count(it, HALF + (t | 1)) + 1)
                        wide = -(-cols(t, u) // 256) * 256
                        for c0 in range(0, wide, 512):
                            c1 = min(wide, c0 + 512)
                            masked = c0 <= i * P < c1
                            for n, (qp, kp) in enumerate(((0, 0), (0, 1), (1, 0))):
                                last = pe.matmul(s_ps[:, slot, c0:c1], qk[:, qp, h, i * P:(i + 1) * P], qk[:, kp, REP, c0:c1],
                                                 start=n == 0, stop=n == 2 and not masked)
                            if masked:
                                last = pe.matmul(s_ps[:, slot, i * P:(i + 1) * P], identb[:, :], maskb[:, :],
                                                 start=False, stop=True)
                        last.then_inc(s_done, 1)
                    if kind == "T":
                        u, j = a
                        k = blocks_before(u) + j
                        if j == 0:
                            pe.wait_ge(p_done, it * UNITS * QT + (u + 1) * QT)
                        if k >= 2:
                            pe.wait_ge(ptlo_done, it * BLOCKS + k - 1)
                        for t in range(first_col(u, j) // P, QT):
                            seen = j <= QT * (u // REP) + t
                            src = weights(u, t, j * P, (j + 1) * P) if seen else zeros[:, :]
                            last = pe.transpose(t_ps[:, k % 2, t * P:(t + 1) * P], src, ident[:, :])
                        last.then_inc(pt_turned, 1)
                    if kind == "PV":
                        u, j = a
                        k, c = blocks_before(u) + j, first_col(u, j)
                        pe.wait_ge(ptlo_done, it * BLOCKS + k + 1)
                        if j == 0:
                            if u == 0:
                                pe.wait_ge(added, 1 + it * NST)
                                pe.wait_ge(vhi_moved, it + 1)
                                pe.wait_ge(vlo_moved, it + 1)
                            if u == REP + 1:
                                pe.wait_ge(added, 1 + it * NST + QT)
                            if u >= 2:
                                pe.wait_ge(alo_done, it * UNITS + u - 1)
                        for n, (vp, pp) in enumerate(((0, 0), (0, 1), (1, 0))):
                            last = pe.matmul(o_ps[:, u % 2, c:], v[:, vp, j, :], pT[:, k % PT_RING, pp, c:],
                                             start=j == 0 and n == 0, stop=j == blocks_of(u) - 1 and n == 2)
                        if j == blocks_of(u) - 1:
                            last.then_inc(pv_done, 1)
                        elif (u, j) == (UNITS - 1, HALF - 1):
                            last.then_inc(v_free, 1)
                    if kind == "out":
                        i, = a
                        if i == 0:
                            pe.wait_ge(wo_in, (it + 1) * (16 * REP))
                            pe.wait_ge(alo_done, it * UNITS + REP)
                        elif i < QT:
                            pe.wait_ge(added, 1 + it * NST + i)
                        elif i == QT:
                            pe.wait_ge(alo_done, it * UNITS + UNITS)
                        elif i >= QT + 2:
                            pe.wait_ge(added, 1 + it * NST + i - 1)
                        t = i % QT
                        for h in range(REP):
                            for ap, wp in ((0, 0), (0, 1), (1, 0)):
                                last = pe.matmul(o_ps[:, out_bank(i), :], aT[:, ap, h, t * P:(t + 1) * P], woT[:, wp, h, :],
                                                 start=h == 0 and ap == wp == 0, stop=h == REP - 1 and ap == 1)
                        last.then_inc(out_done, 1)

            every_head(pe, body)


INPUTS = {"x": "L0_attn_x", "wqkv": "L0_attn_w_qkv", "wo": "L0_attn_w_o", "wg": "L0_ffn_wq_gate",
          "wu": "L0_ffn_wq_up", "wd": "L0_ffn_wq_down", "sg": "L0_ffn_s_gate", "su": "L0_ffn_s_up",
          "sd": "L0_ffn_s_down", "qg": "L0_attn_qn_g", "qb": "L0_attn_qn_b", "kg": "L0_attn_kn_g", "kb": "L0_attn_kn_b"}
NORMS = ("qg", "qb", "kg", "kb")


def build_program(nc, t, out):
    xT = nc.dram_tensor("xT_scratch", [TG, P, TPG, 2, KC, P], F32, kind="Internal").ap()
    wqkvT = nc.dram_tensor("wqkvT_scratch", [QKV_TILES, P, 2, KC, P], F32, kind="Internal").ap()
    woT = nc.dram_tensor("woT_scratch", [H, P, 2, KC, P], F32, kind="Internal").ap()
    gate = nc.dram_tensor("gate_scratch", [TILES, P, DIM], F32, kind="Internal").ap()
    x = t["x"].rearrange("b (t p) n -> (b t) p n", p=P)
    ffn_dram = {
        "x": x,
        "wqkv": t["wqkv"].rearrange("(r p) n -> r p n", p=P),
        "wo": t["wo"].rearrange("(r p) (h j) -> h p r j", p=P, j=P),
        "wg": t["wg"].rearrange("(c p) n -> c p n", p=P),
        "wu": t["wu"].rearrange("(c p) n -> c p n", p=P),
        "wd": t["wd"].rearrange("(r p) (c j) -> c p r j", p=P, j=P),
        "sg": t["sg"], "su": t["su"], "sd": t["sd"],
    }
    ffn_block(nc, ffn_dram, (xT, wqkvT, woT, gate))
    attention_block(nc, {"x": x, "cos": t["cos"], "ssin": t["ssin"], "norms": [t[n] for n in NORMS]},
                    (xT, wqkvT, woT.rearrange("h p a c n -> h p a (c n)"), gate),
                    out.rearrange("b (t p) n -> (b t) p n", p=P))


def kernel(**inputs):
    import numpy as np
    from concourse import bacc
    from concourse.bass_utils import run_bass_kernel_spmd

    arrays = {short: np.ascontiguousarray(inputs[name]) for short, name in INPUTS.items()}
    inv_freq = (1.0 / np.float32(1000000.0) ** (np.arange(0, D, 2, dtype=np.float32) / np.float32(D))).astype(np.float32)
    freqs = np.outer(np.arange(S, dtype=np.float32), inv_freq).astype(np.float32)
    cos, sin = np.cos(freqs.astype(np.float64)), np.sin(freqs.astype(np.float64))
    tiles = lambda a: np.ascontiguousarray(a.astype(np.float32).reshape(NST, P, -1).transpose(1, 0, 2))
    arrays["cos"] = tiles(cos)
    arrays["ssin"] = tiles(np.concatenate([-sin, sin], 1))

    nc = bacc.Bacc("TRN2", target_bir_lowering=False, num_devices=1)
    handles = {k: nc.dram_tensor(f"in_{k}", a.shape, mybir.dt.from_np(a.dtype), kind="ExternalInput").ap()
               for k, a in arrays.items()}
    out = nc.dram_tensor("out_x", (B, S, DIM), F32, kind="ExternalOutput").ap()
    build_program(nc, handles, out)
    r = run_bass_kernel_spmd(nc, [{f"in_{k}": a for k, a in arrays.items()}], core_ids=[0])
    return r.results[0]["out_x"]
```
